# Optimizing a Trainium2 kernel written in Bass

```python
import numpy as np
import jax
import jax.numpy as jnp

def _softmax(x, axis=-1):
    return jax.nn.softmax(x, axis=axis)

def _gelu(x):
    return jax.nn.gelu(x, approximate=True)

def _silu(x):
    return jax.nn.silu(x)

def _sigmoid(x):
    return jax.nn.sigmoid(x)

def _layernorm(x, axis=-1, eps=1e-05):
    m = jnp.mean(x, axis=axis, keepdims=True)
    v = jnp.var(x, axis=axis, keepdims=True)
    return (x - m) / jnp.sqrt(v + eps)

def _scatter_add(tgt, idx, src, axis=0):
    return tgt.at[idx].add(src)

def _segment_sum(src, seg, n):
    return jax.ops.segment_sum(src, seg, n)
kernel_name = 'mk_seq_postln_d2_jaxref_r8_ea76f7'

def setup_inputs(seed: int=0):
    np.random.seed(seed)
    _w = jnp.asarray

    def _L0_attn_setup():
        import jax, jax.numpy as jnp
        import numpy as np
        import math
        B, S, E, H = (2, 256, 128, 8)
        Dh = E // H

        def _pos_encoding(s, e):
            pos = jnp.arange(s, dtype=jnp.float32)[:, None]
            div = jnp.exp(jnp.arange(0, e, 2, dtype=jnp.float32) * (-math.log(10000.0) / e))
            pe = jnp.zeros((s, e), jnp.float32)
            pe = pe.at[:, 0::2].set(jnp.sin(pos * div))
            pe = pe.at[:, 1::2].set(jnp.cos(pos * div))
            return pe

        def _rel_shift(ps):
            b, h, s1, s2 = ps.shape
            padded = jnp.pad(ps, ((0, 0), (0, 0), (0, 0), (1, 0)))
            return padded.reshape(b, h, s2 + 1, s1)[:, :, 1:, :].reshape(b, h, s1, s2)

        def _forward(inputs, ln_gamma, ln_beta, Wq, bq, Wk, bk, Wv, bv, Wp, u_bias, v_bias, Wo, bo):
            b, s, e = inputs.shape
            mu = inputs.mean(-1, keepdims=True)
            var = inputs.var(-1, keepdims=True)
            xn = (inputs - mu) / jnp.sqrt(var + 1e-05) * ln_gamma + ln_beta
            xh = xn.reshape(b, s, H, Dh)
            q = xh @ Wq + bq
            k = xh @ Wk + bk
            v = xh @ Wv + bv
            pe = _pos_encoding(s, e).reshape(s, H, Dh)
            p = pe @ Wp
            content = jnp.einsum('bqhd,bkhd->bhqk', q + u_bias, k)
            pos_score = jnp.einsum('bqhd,khd->bhqk', q + v_bias, p)
            pos_score = _rel_shift(pos_score)
            score = (content + pos_score) / jnp.sqrt(jnp.float32(e))
            attn = jax.nn.softmax(score, axis=-1)
            ctx = jnp.einsum('bhqk,bkhd->bqhd', attn, v).reshape(b, s, e)
            return ctx @ Wo + bo
        key = jax.random.key(seed)
        ks = jax.random.split(key, 9)
        g = lambda k, shp: jax.random.normal(k, shp, jnp.float32) * 0.02
        return {'inputs': jax.random.normal(ks[0], (B, S, E), jnp.float32), 'ln_gamma': jnp.ones((E,), jnp.float32), 'ln_beta': jnp.zeros((E,), jnp.float32), 'Wq': g(ks[1], (Dh, Dh)), 'bq': jnp.zeros((Dh,), jnp.float32), 'Wk': g(ks[2], (Dh, Dh)), 'bk': jnp.zeros((Dh,), jnp.float32), 'Wv': g(ks[3], (Dh, Dh)), 'bv': jnp.zeros((Dh,), jnp.float32), 'Wp': g(ks[4], (Dh, Dh)), 'u_bias': g(ks[5], (H, Dh)), 'v_bias': g(ks[6], (H, Dh)), 'Wo': g(ks[7], (E, E)), 'bo': jnp.zeros((E,), jnp.float32)}
    _L0_attn_in = _L0_attn_setup()

    def _L0_ffn_setup():
        import jax, jax.numpy as jnp
        import numpy as np
        B, T, D, F, E = (2, 128, 128, 512, 8)
        EPS = 1e-06
        key = jax.random.key(seed)
        k = jax.random.split(key, 5)
        scale = 0.02
        return {'x': jax.random.normal(k[0], (B, T, D), dtype=jnp.float32), 'rms_w': jnp.ones((D,), dtype=jnp.float32), 'gate_w': jax.random.normal(k[1], (E, D), dtype=jnp.float32) * scale, 'W1': jax.random.normal(k[2], (E, D, F), dtype=jnp.float32) * scale, 'b1': jnp.zeros((E, F), dtype=jnp.float32), 'W2': jax.random.normal(k[3], (E, F, D), dtype=jnp.float32) * scale, 'b2': jnp.zeros((E, D), dtype=jnp.float32)}
    _L0_ffn_in = _L0_ffn_setup()

    def _L1_attn_setup():
        import jax, jax.numpy as jnp
        import numpy as np
        from jax import lax
        D_MODEL = 128
        INNER = 256
        K = 3
        B, S = (4, 256)

        def _layernorm(x, gamma, beta, eps=1e-05):
            mu = jnp.mean(x, axis=-1, keepdims=True)
            var = jnp.mean(jnp.square(x - mu), axis=-1, keepdims=True)
            return (x - mu) * lax.rsqrt(var + eps) * gamma + beta

        def _forward(x, W_in, b_in, conv_w, conv_b, Wa, ba, Wb, bb, Wc, bc, Wo, bo, gamma, beta):
            residual = x
            xn = _layernorm(x, gamma, beta)
            proj = xn @ W_in + b_in
            projected, gate = jnp.split(proj, 2, axis=-1)
            conv_in = jnp.swapaxes(projected, 1, 2)
            conv_out = lax.conv_general_dilated(conv_in, conv_w, window_strides=(1,), padding=[(K - 1, 0)], feature_group_count=INNER, dimension_numbers=('NCH', 'OIH', 'NCH'))
            conv_out = jnp.swapaxes(conv_out + conv_b[None, :, None], 1, 2)
            u = jax.nn.silu(conv_out) * jax.nn.sigmoid(gate)
            a = jax.nn.sigmoid(u @ Wa + ba)
            b = jax.nn.sigmoid(u @ Wb + bb)
            c = jnp.tanh(u @ Wc + bc)

            def step(state, abu):
                a_t, b_t, c_t, u_t = abu
                state = a_t * state + b_t * u_t
                return (state, c_t * state + u_t)
            seq = tuple((jnp.swapaxes(t, 0, 1) for t in (a, b, c, u)))
            _, y = lax.scan(step, jnp.zeros((x.shape[0], INNER), x.dtype), seq)
            y = jnp.swapaxes(y, 0, 1)
            return residual + y @ Wo + bo
        key = jax.random.key(seed)
        ks = jax.random.split(key, 8)
        s = 0.02
        return {'x': jax.random.normal(ks[0], (B, S, D_MODEL), dtype=jnp.float32), 'W_in': jax.random.normal(ks[1], (D_MODEL, 2 * INNER), dtype=jnp.float32) * s, 'b_in': jnp.zeros((2 * INNER,), jnp.float32), 'conv_w': jax.random.normal(ks[2], (INNER, 1, K), dtype=jnp.float32) * s, 'conv_b': jnp.zeros((INNER,), jnp.float32), 'Wa': jax.random.normal(ks[3], (INNER, INNER), dtype=jnp.float32) * s, 'ba': jnp.zeros((INNER,), jnp.float32), 'Wb': jax.random.normal(ks[4], (INNER, INNER), dtype=jnp.float32) * s, 'bb': jnp.zeros((INNER,), jnp.float32), 'Wc': jax.random.normal(ks[5], (INNER, INNER), dtype=jnp.float32) * s, 'bc': jnp.zeros((INNER,), jnp.float32), 'Wo': jax.random.normal(ks[6], (INNER, D_MODEL), dtype=jnp.float32) * s, 'bo': jnp.zeros((D_MODEL,), jnp.float32), 'gamma': jnp.ones((D_MODEL,), jnp.float32), 'beta': jnp.zeros((D_MODEL,), jnp.float32)}
    _L1_attn_in = _L1_attn_setup()

    def _L1_ffn_setup():
        import jax, jax.numpy as jnp
        import numpy as np
        B, S, D, E, F = (2, 256, 128, 14, 256)
        key = jax.random.key(seed)
        k = jax.random.split(key, 4)
        h = jax.random.normal(k[0], (B, S, D), dtype=jnp.float32)
        router_w = jax.random.normal(k[1], (D, E), dtype=jnp.float32) * 0.02
        w1 = jax.random.uniform(k[2], (E, D, F), dtype=jnp.float32, minval=-1.0, maxval=1.0) * float(np.sqrt(6.0 / D))
        w2 = jax.random.uniform(k[3], (E, F, D), dtype=jnp.float32, minval=-1.0, maxval=1.0) * float(np.sqrt(6.0 / F))
        b1 = jnp.zeros((E, F), dtype=jnp.float32)
        b2 = jnp.zeros((E, D), dtype=jnp.float32)
        return {'h': h, 'router_w': router_w, 'w1': w1, 'b1': b1, 'w2': w2, 'b2': b2}
    _L1_ffn_in = _L1_ffn_setup()
    _d = {'L0_attn_inputs': _L0_attn_in['inputs'], 'L0_attn_ln_gamma': _L0_attn_in['ln_gamma'], 'L0_attn_ln_beta': _L0_attn_in['ln_beta'], 'L0_attn_Wq': _L0_attn_in['Wq'], 'L0_attn_bq': _L0_attn_in['bq'], 'L0_attn_Wk': _L0_attn_in['Wk'], 'L0_attn_bk': _L0_attn_in['bk'], 'L0_attn_Wv': _L0_attn_in['Wv'], 'L0_attn_bv': _L0_attn_in['bv'], 'L0_attn_Wp': _L0_attn_in['Wp'], 'L0_attn_u_bias': _L0_attn_in['u_bias'], 'L0_attn_v_bias': _L0_attn_in['v_bias'], 'L0_attn_Wo': _L0_attn_in['Wo'], 'L0_attn_bo': _L0_attn_in['bo'], 'L0_ffn_rms_w': _L0_ffn_in['rms_w'], 'L0_ffn_gate_w': _L0_ffn_in['gate_w'], 'L0_ffn_W1': _L0_ffn_in['W1'], 'L0_ffn_b1': _L0_ffn_in['b1'], 'L0_ffn_W2': _L0_ffn_in['W2'], 'L0_ffn_b2': _L0_ffn_in['b2'], 'L1_attn_W_in': _L1_attn_in['W_in'], 'L1_attn_b_in': _L1_attn_in['b_in'], 'L1_attn_conv_w': _L1_attn_in['conv_w'], 'L1_attn_conv_b': _L1_attn_in['conv_b'], 'L1_attn_Wa': _L1_attn_in['Wa'], 'L1_attn_ba': _L1_attn_in['ba'], 'L1_attn_Wb': _L1_attn_in['Wb'], 'L1_attn_bb': _L1_attn_in['bb'], 'L1_attn_Wc': _L1_attn_in['Wc'], 'L1_attn_bc': _L1_attn_in['bc'], 'L1_attn_Wo': _L1_attn_in['Wo'], 'L1_attn_bo': _L1_attn_in['bo'], 'L1_attn_gamma': _L1_attn_in['gamma'], 'L1_attn_beta': _L1_attn_in['beta'], 'L1_ffn_router_w': _L1_ffn_in['router_w'], 'L1_ffn_w1': _L1_ffn_in['w1'], 'L1_ffn_b1': _L1_ffn_in['b1'], 'L1_ffn_w2': _L1_ffn_in['w2'], 'L1_ffn_b2': _L1_ffn_in['b2']}
    _x0 = _d['L0_attn_inputs']
    _d['L0_attn_inputs'] = jax.random.normal(jax.random.fold_in(jax.random.key(seed), 1), (4, 512, 128), dtype=_x0.dtype)
    del _x0
    return _d

def reference(L0_attn_inputs, L0_attn_ln_gamma, L0_attn_ln_beta, L0_attn_Wq, L0_attn_bq, L0_attn_Wk, L0_attn_bk, L0_attn_Wv, L0_attn_bv, L0_attn_Wp, L0_attn_u_bias, L0_attn_v_bias, L0_attn_Wo, L0_attn_bo, L0_ffn_rms_w, L0_ffn_gate_w, L0_ffn_W1, L0_ffn_b1, L0_ffn_W2, L0_ffn_b2, L1_attn_W_in, L1_attn_b_in, L1_attn_conv_w, L1_attn_conv_b, L1_attn_Wa, L1_attn_ba, L1_attn_Wb, L1_attn_bb, L1_attn_Wc, L1_attn_bc, L1_attn_Wo, L1_attn_bo, L1_attn_gamma, L1_attn_beta, L1_ffn_router_w, L1_ffn_w1, L1_ffn_b1, L1_ffn_w2, L1_ffn_b2):

    def _L0_attn_ref(inputs, ln_gamma, ln_beta, Wq, bq, Wk, bk, Wv, bv, Wp, u_bias, v_bias, Wo, bo):
        import jax, jax.numpy as jnp
        import numpy as np
        import math
        B, S, E, H = (2, 256, 128, 8)
        Dh = E // H

        def _pos_encoding(s, e):
            pos = jnp.arange(s, dtype=jnp.float32)[:, None]
            div = jnp.exp(jnp.arange(0, e, 2, dtype=jnp.float32) * (-math.log(10000.0) / e))
            pe = jnp.zeros((s, e), jnp.float32)
            pe = pe.at[:, 0::2].set(jnp.sin(pos * div))
            pe = pe.at[:, 1::2].set(jnp.cos(pos * div))
            return pe

        def _rel_shift(ps):
            b, h, s1, s2 = ps.shape
            padded = jnp.pad(ps, ((0, 0), (0, 0), (0, 0), (1, 0)))
            return padded.reshape(b, h, s2 + 1, s1)[:, :, 1:, :].reshape(b, h, s1, s2)

        def _forward(inputs, ln_gamma, ln_beta, Wq, bq, Wk, bk, Wv, bv, Wp, u_bias, v_bias, Wo, bo):
            b, s, e = inputs.shape
            mu = inputs.mean(-1, keepdims=True)
            var = inputs.var(-1, keepdims=True)
            xn = (inputs - mu) / jnp.sqrt(var + 1e-05) * ln_gamma + ln_beta
            xh = xn.reshape(b, s, H, Dh)
            q = xh @ Wq + bq
            k = xh @ Wk + bk
            v = xh @ Wv + bv
            pe = _pos_encoding(s, e).reshape(s, H, Dh)
            p = pe @ Wp
            content = jnp.einsum('bqhd,bkhd->bhqk', q + u_bias, k)
            pos_score = jnp.einsum('bqhd,khd->bhqk', q + v_bias, p)
            pos_score = _rel_shift(pos_score)
            score = (content + pos_score) / jnp.sqrt(jnp.float32(e))
            attn = jax.nn.softmax(score, axis=-1)
            ctx = jnp.einsum('bhqk,bkhd->bqhd', attn, v).reshape(b, s, e)
            return ctx @ Wo + bo
        return _forward(inputs, ln_gamma, ln_beta, Wq, bq, Wk, bk, Wv, bv, Wp, u_bias, v_bias, Wo, bo)

    def _L0_ffn_ref(x, rms_w, gate_w, W1, b1, W2, b2):
        import jax, jax.numpy as jnp
        import numpy as np
        B, T, D, F, E = (2, 128, 128, 512, 8)
        EPS = 1e-06
        ms = jnp.mean(x * x, axis=-1, keepdims=True)
        xn = x * jax.lax.rsqrt(ms + EPS) * rms_w
        logits = jnp.einsum('btd,ed->bte', xn, gate_w)
        scores = jax.nn.softmax(logits, axis=-1)
        top1_idx = jnp.argmax(scores, axis=-1)
        top1_score = jnp.max(scores, axis=-1)
        out = jnp.zeros_like(xn)
        for e in range(E):
            h = jax.nn.silu(jnp.einsum('btd,df->btf', xn, W1[e]) + b1[e])
            ye = jnp.einsum('btf,fd->btd', h, W2[e]) + b2[e]
            out = jnp.where((top1_idx == e)[..., None], ye, out)
        return out * top1_score[..., None]

    def _L1_attn_ref(x, W_in, b_in, conv_w, conv_b, Wa, ba, Wb, bb, Wc, bc, Wo, bo, gamma, beta):
        import jax, jax.numpy as jnp
        import numpy as np
        from jax import lax
        D_MODEL = 128
        INNER = 256
        K = 3
        B, S = (4, 256)

        def _layernorm(x, gamma, beta, eps=1e-05):
            mu = jnp.mean(x, axis=-1, keepdims=True)
            var = jnp.mean(jnp.square(x - mu), axis=-1, keepdims=True)
            return (x - mu) * lax.rsqrt(var + eps) * gamma + beta

        def _forward(x, W_in, b_in, conv_w, conv_b, Wa, ba, Wb, bb, Wc, bc, Wo, bo, gamma, beta):
            residual = x
            xn = _layernorm(x, gamma, beta)
            proj = xn @ W_in + b_in
            projected, gate = jnp.split(proj, 2, axis=-1)
            conv_in = jnp.swapaxes(projected, 1, 2)
            conv_out = lax.conv_general_dilated(conv_in, conv_w, window_strides=(1,), padding=[(K - 1, 0)], feature_group_count=INNER, dimension_numbers=('NCH', 'OIH', 'NCH'))
            conv_out = jnp.swapaxes(conv_out + conv_b[None, :, None], 1, 2)
            u = jax.nn.silu(conv_out) * jax.nn.sigmoid(gate)
            a = jax.nn.sigmoid(u @ Wa + ba)
            b = jax.nn.sigmoid(u @ Wb + bb)
            c = jnp.tanh(u @ Wc + bc)

            def step(state, abu):
                a_t, b_t, c_t, u_t = abu
                state = a_t * state + b_t * u_t
                return (state, c_t * state + u_t)
            seq = tuple((jnp.swapaxes(t, 0, 1) for t in (a, b, c, u)))
            _, y = lax.scan(step, jnp.zeros((x.shape[0], INNER), x.dtype), seq)
            y = jnp.swapaxes(y, 0, 1)
            return residual + y @ Wo + bo
        return _forward(x, W_in, b_in, conv_w, conv_b, Wa, ba, Wb, bb, Wc, bc, Wo, bo, gamma, beta)

    def _L1_ffn_ref(h, router_w, w1, b1, w2, b2):
        import jax, jax.numpy as jnp
        import numpy as np
        B, S, D, E, F = (2, 256, 128, 14, 256)
        Bb, Ss, Dd = h.shape
        x = h.reshape(-1, Dd)
        logits = x @ router_w
        assignments = jnp.argmax(logits, axis=-1)
        probs = jax.nn.softmax(logits, axis=-1)
        weights = jnp.take_along_axis(probs, assignments[:, None], axis=1)[:, 0]
        hid = jnp.einsum('nd,edf->nef', x, w1) + b1
        hid = jax.nn.gelu(hid, approximate=False)
        all_out = jnp.einsum('nef,efd->ned', hid, w2) + b2
        sel = jnp.take_along_axis(all_out, assignments[:, None, None], axis=1)[:, 0, :]
        moe_out = (sel * weights[:, None]).reshape(Bb, Ss, Dd)
        return moe_out
    x = L0_attn_inputs
    x = _layernorm(x + _L0_attn_ref(x, L0_attn_ln_gamma, L0_attn_ln_beta, L0_attn_Wq, L0_attn_bq, L0_attn_Wk, L0_attn_bk, L0_attn_Wv, L0_attn_bv, L0_attn_Wp, L0_attn_u_bias, L0_attn_v_bias, L0_attn_Wo, L0_attn_bo), axis=-1)
    x = _layernorm(x + _L0_ffn_ref(x, L0_ffn_rms_w, L0_ffn_gate_w, L0_ffn_W1, L0_ffn_b1, L0_ffn_W2, L0_ffn_b2), axis=-1)
    x = _layernorm(x + _L1_attn_ref(x, L1_attn_W_in, L1_attn_b_in, L1_attn_conv_w, L1_attn_conv_b, L1_attn_Wa, L1_attn_ba, L1_attn_Wb, L1_attn_bb, L1_attn_Wc, L1_attn_bc, L1_attn_Wo, L1_attn_bo, L1_attn_gamma, L1_attn_beta), axis=-1)
    x = _layernorm(x + _L1_ffn_ref(x, L1_ffn_router_w, L1_ffn_w1, L1_ffn_b1, L1_ffn_w2, L1_ffn_b2), axis=-1)
    return x

_drawn_inputs = setup_inputs


def setup_inputs(seed=0):
    import zlib

    import numpy as np

    out = dict(_drawn_inputs(seed))
    spreads = {'L0_attn_ln_gamma': (1.0, 0.6),
     'L0_attn_ln_beta': (0.0, 0.8),
     'L0_attn_bq': (0.0, 0.8),
     'L0_attn_bk': (0.0, 2.0),
     'L0_attn_bv': (0.0, 0.1),
     'L0_attn_bo': (0.0, 0.1),
     'L0_ffn_rms_w': (1.0, 0.6),
     'L0_ffn_b1': (0.0, 0.704),
     'L0_ffn_b2': (0.0, 0.1),
     'L1_attn_b_in': (0.0, 0.8),
     'L1_attn_conv_b': (0.0, 0.8),
     'L1_attn_ba': (0.0, 0.8),
     'L1_attn_bb': (0.0, 0.8),
     'L1_attn_bc': (0.0, 0.8),
     'L1_attn_bo': (0.0, 0.1),
     'L1_attn_gamma': (1.0, 0.6),
     'L1_attn_beta': (0.0, 0.8),
     'L1_ffn_b1': (0.0, 0.755),
     'L1_ffn_b2': (0.0, 0.766)}
    factors = {'L0_attn_Wq': 8.0,
     'L0_attn_Wk': 8.0,
     'L0_attn_Wv': 8.0,
     'L0_attn_Wp': 47.888,
     'L0_attn_u_bias': 22.594,
     'L0_attn_v_bias': 64.0,
     'L0_ffn_W1': 3.617,
     'L0_ffn_W2': 3.299,
     'L1_attn_W_in': 8.0,
     'L1_attn_conv_w': 8.0,
     'L1_attn_Wa': 8.0,
     'L1_attn_Wb': 8.0,
     'L1_attn_Wc': 8.0,
     'L1_attn_Wo': 6.309}
    for name, (base, spread) in spreads.items():
        noise = np.random.default_rng([zlib.crc32(name.encode()), seed]).standard_normal(out[name].shape)
        drawn = base * np.exp(spread * noise) if base else spread * noise
        out[name] = jnp.asarray(drawn.astype(out[name].dtype))
    for name, factor in factors.items():
        out[name] = (out[name] * factor).astype(out[name].dtype)
    return out
```

```python
from contextlib import ExitStack

import numpy as np

import concourse.bass as bass
from concourse import mybir
from concourse.alu_op_type import AluOpType as ALU

F32 = mybir.dt.float32
I32 = mybir.dt.int32
U32 = mybir.dt.uint32
ACT = mybir.ActivationFunctionType
AX = mybir.AxisListType

P = 128
B, S, D = 4, 512, 128
TB = S // P
NTOK = B * TB
H, DH = 8, 16
HG = 4
NG = H // HG
SCALE = float(D) ** -0.5
E0, F0 = 8, 512
E1, F1 = 14, 256
INNER = 256
NC = INNER // P
RING = 3


def slot_tiles(experts):
    most = (B * S + experts * (P - 1)) // P
    return -(-most // RING) * RING


NT0, NT1 = slot_tiles(E0), slot_tiles(E1)
WW0 = F0 + F0 + F0 // P + D
WW1 = F1 + F1 + F1 // P + D


def columns(fields):
    at, out = 0, {}
    for name, width in fields:
        out[name] = (at, width)
        at += width
    return out, at


FIELDS_A = [("ident", P), ("tri", P), ("wq", P), ("wk0", P), ("wk1", P), ("wv", P), ("m1_0", P), ("m1_1", P),
            ("m2_0", P), ("m2_1", P), ("wp", P), ("pem", H), ("gamma", 1), ("beta", 1), ("bq", 1), ("v", 1), ("pmask", 2),
            ("bk0", 1), ("bk1", 1), ("u0", 1), ("u1", 1), ("v0", 1), ("v1", 1), ("bv", D), ("bo", D), ("wo", D)]
FIELDS_T = [("cos0", S), ("cos1", S), ("sin0", S), ("sin1", S), ("ka0", S), ("ka1", S), ("kb0", S), ("kb1", S)]
FIELDS_B = [("upper", P), ("ones", P), ("rms", D), ("gate", E0), ("router", E1), ("bo1", D),
            ("rev0", NTOK * E0), ("rev1", NTOK * E1), ("run0", NTOK * E0), ("run1", NTOK * E1),
            ("thr0", NTOK * E0), ("thr1", NTOK * E1), ("slot0", NT0 * E0), ("slot1", NT1 * E1),
            ("gamma1", 1), ("beta1", 1), ("win", 2 * INNER), ("bin", 2 * NC), ("cw", NC * 3), ("cb", NC),
            ("wa", NC * INNER), ("wb", NC * INNER), ("wc", NC * INNER), ("ba", NC), ("bb", NC), ("bc", NC),
            ("wo1", NC * D)]
COL_A, WIDE_A = columns(FIELDS_A)
COL_T, WIDE_T = columns(FIELDS_T)
COL_B, WIDE_B = columns(FIELDS_B)


def plan_attention():
    jobs, plan = [], []

    def job(name, *where):
        jobs.append((name, *where))
        plan.append(("job", len(jobs) - 1))

    def projections(b):
        return [("stats", b), ("normz", b), ("job", "zT", b), ("job", "q", b), ("job", "k", b, 0), ("job", "k", b, 1),
                ("job", "v", b), ("job", "t1", b, 0), ("job", "t2", b, 0), ("job", "t1", b, 1),
                ("job", "t2", b, 1), ("job", "corr", b)]

    def put(event):
        if event[0] == "job":
            job(*event[1:])
        else:
            plan.append(event)

    put(("job", "pem", 0))
    for e in projections(0):
        put(e)
    units = B * TB * H
    waiting = {}
    per = TB * H
    for b in range(1, B):
        for n, e in enumerate(projections(b)):
            waiting.setdefault((b - 1) * per + 2 * n + (2 if n == 0 else 6), []).append(e)
    for n in range(NTOK):
        at = H * (n + 1)
        waiting.setdefault(at + 1, []).append(("norm", n))
        waiting.setdefault(at + 2, []).append(("job", "ctxT", n))
        waiting.setdefault(at + 4, []).append(("job", "out", n))
        if n % TB == TB - 1:
            b = n // TB
            waiting.setdefault(at + 5, []).append(("post", b))
            waiting.setdefault(at + 8, []).append(("post2", b))
            waiting.setdefault(at + 11, []).append(("rms", b))
            waiting.setdefault(at + 12, []).append(("job", "xT", b))
            waiting.setdefault(at + 14, []).append(("job", "logits", b))
    plan.append(("score", 0))
    plan.append(("score", 1))
    for u in range(units + 16):
        if u < units:
            plan.append(("probs", u))
        if u + 2 < units:
            plan.append(("score", u + 2))
        for e in waiting.pop(u, []):
            put(e)
        if 1 <= u <= units:
            plan.append(("values", u - 1))
    assert not waiting, waiting
    return jobs, plan


def plan_recurrence():
    steps = [("P", 0)]
    for b in range(B):
        if b + 1 < B:
            steps.append(("P", b + 1))
        steps.append(("G", b))
        steps.append(("O", b))
    return steps


def build(nc, x_in, ca_in, ct_in, cb_in, wp0_in, wp1_in, out):
    jobs, plan = plan_attention()
    number = {j: k for k, j in enumerate(jobs)}
    power = {e: k + 1 for k, e in enumerate(e for e in plan if e[0] in ("stats", "post", "rms"))}
    variance = {e: k + 1 for k, e in enumerate(e for e in plan if e[0] in ("stats", "post"))}

    xs = [nc.dram_tensor(f"slots_in_{l}", (n * P, D), F32, kind="Internal").ap() for l, n in ((0, NT0), (1, NT1))]
    ys = [nc.dram_tensor(f"slots_out_{l}", (n * P, D), F32, kind="Internal").ap() for l, n in ((0, NT0), (1, NT1))]
    x_view = x_in.rearrange("b (t p) d -> p (b t) d", p=P)
    out_view = out.rearrange("b (t p) d -> p (b t) d", p=P)

    with ExitStack() as ctx:
        def sb(name, shape, dt=F32):
            return ctx.enter_context(nc.sbuf_tensor(name, shape, dt))

        def sem(name):
            return ctx.enter_context(nc.semaphore(name))

        bank = [ctx.enter_context(nc.psum_tensor(f"bank{i}", [P, 512], F32)) for i in range(8)]

        ca = sb("ca", [P, WIDE_A])
        cb = sb("cb", [P, WIDE_B])

        def A(name, rows=slice(None)):
            at, w = COL_A[name]
            return ca[rows, at:at + w]

        def C(name, a=0, n=None, rows=slice(None)):
            at, w = COL_B[name]
            return cb[rows, at + a:at + a + (w - a if n is None else n)]

        QW = S + 1
        arena1 = sb("arena1", [P, max(WIDE_T + 2 * NG * (2 * QW + 2 * S), E1 * WW1)])
        ct = arena1[:, 0:WIDE_T]
        rest = arena1[:, WIDE_T:WIDE_T + 2 * NG * (2 * QW + 2 * S)]

        def part(at, w):
            return rest[:, at:at + 2 * NG * w].rearrange("p (r g q) -> p r g q", r=2, g=NG)

        qa = part(0, QW)
        qb = part(2 * NG * QW, S)
        ka = part(2 * NG * (QW + S), S)
        kb = part(2 * NG * (QW + 2 * S), S)
        wp1 = arena1[:, 0:E1 * WW1]

        def T(name):
            at, w = COL_T[name]
            return ct[:, at:at + w]

        PJ = S + 2
        REC = NC * (2 * PJ + 5 * S * 2 + 2 * S)
        arena2 = sb("arena2", [P, max(E0 * WW0, REC)])
        wp0 = arena2[:, 0:E0 * WW0]

        xa = sb("xa", [P, NTOK, D])
        xb = sb("xb", [P, NTOK, D])
        xc = sb("xc", [P, NTOK, D])
        z = sb("z", [P, TB, D])
        xnT = sb("xnT", [P, S])
        qvT = sb("qvT", [P, 2, QW])
        vv = sb("vv", [P, 2, TB, D])
        corr = sb("corr", [P, 2, TB, H])
        t1 = sb("t1", [P, S])
        t2 = sb("t2", [P, S])
        work = sb("work", [P, 4 * S])
        prob = work[:, 0:2 * S].rearrange("p (r k) -> p r k", r=2)
        probT = work[:, 2 * S:4 * S].rearrange("p (r k) -> p r k", r=2)
        hT = work[:, 0:RING * F0].rearrange("p (r f) -> p r f", r=RING)
        yb = work[:, RING * F0:RING * (F0 + D)].rearrange("p (r d) -> p r d", r=RING)
        cn = sb("cn", [P, D])
        cT = sb("cT", [P, P])
        col = sb("col", [P, 8])
        pm1 = sb("pm1", [P, H])
        nmax = sb("nmax", [P, 2, 1])
        rsum = sb("rsum", [P, 2, H])
        rinv = sb("rinv", [P, H])
        st = sb("st", [P, TB, 6])
        mv = sb("mv", [P, 2, TB, 2])
        rstd = sb("rstd", [P, 3, TB])
        half = sb("half", [P, NTOK])
        junk = sb("junk", [P, D])
        xnT2 = sb("xnT2", [P, S])
        slotcmp = t1[0:1, :]
        ssq = sb("ssq", [P, NTOK])
        zeros = sb("zeros", [P, 512])
        lg = sb("lg", [P, NTOK * E1])
        rt = [sb(f"rt{i}", [P, NTOK * E1]) for i in range(5)]
        sm = sb("sm", [P, 6, NTOK])
        pos = sb("pos", [P, NTOK], I32)
        tex = sb("tex", [1, NT1])
        offs = sb("offs", [1, NT1], I32)
        wbuf = sb("wbuf", [P, RING, max(WW0, WW1)])
        xt = sb("xt", [P, RING, D])
        xTs = t2[:, 0:RING * P].rearrange("p (r q) -> p r q", r=RING)

        rec_at = [0]

        def rec(*dims):
            n = int(np.prod(dims))
            v = arena2[:, rec_at[0]:rec_at[0] + n]
            rec_at[0] += n
            names = "abc"[:len(dims)]
            return v.rearrange(f"p ({' '.join(names)}) -> p {' '.join(names)}", **{k: d for k, d in zip(names, dims)})

        pj = rec(2, NC, PJ)
        sg = rec(2, NC, S)
        uu = rec(2, NC, S)
        ga = rec(2, NC, S)
        gb = rec(2, NC, S)
        gc = rec(2, NC, S)
        cv = rec(NC, S)
        sc = rec(NC, S)
        assert rec_at[0] <= REC

        s_x = [sem(f"s_xin{k}") for k in range(2)]
        s_ca = sem("s_ca")
        s_ct = sem("s_ct")
        s_cb = sem("s_cb")
        s_w0 = sem("s_w0")
        s_w1 = sem("s_w1")
        s_zs = sem("s_zs")
        s_z = sem("s_z")
        s_x1 = sem("s_x1")
        s_xn2 = sem("s_xn2")
        s_xbo = sem("s_xbo")
        s_set = sem("s_set")
        s_pow = sem("s_pow")
        s_gstep = sem("s_gstep")
        s_v = sem("s_v")
        s_score = sem("s_score")
        s_fixed = sem("s_fixed")
        s_diag = sem("s_diag")
        s_exp = sem("s_exp")
        s_pT = sem("s_pT")
        s_pTs = sem("s_pTs")
        s_pv = sem("s_pv")
        s_job = sem("s_job")
        s_out = sem("s_out")
        s_q = sem("s_q")
        s_norm = sem("s_norm")
        s_var = sem("s_var")
        s_sq = sem("s_sq")
        s_rt = sem("s_rt")
        s_rte = sem("s_rte")
        s_rtp = sem("s_rtp")
        s_disp = [sem(f"s_disp{l}") for l in range(2)]
        s_gath = [[sem(f"s_gath{l}_{b}") for b in range(B)] for l in range(2)]
        s_xload = [[sem(f"s_xload{l}_{r}") for r in range(RING)] for l in range(2)]
        s_ystore = [[sem(f"s_ystore{l}_{r}") for r in range(RING)] for l in range(2)]
        s_xT = [sem(f"s_xT{l}") for l in range(2)]
        s_xTs = [sem(f"s_xTs{l}") for l in range(2)]
        s_wb = [sem(f"s_wb{l}") for l in range(2)]
        s_h = [sem(f"s_h{l}") for l in range(2)]
        s_act = [sem(f"s_act{l}") for l in range(2)]
        s_y = [sem(f"s_y{l}") for l in range(2)]
        s_yb = [sem(f"s_yb{l}") for l in range(2)]
        s_z1 = sem("s_z1")
        s_rzT = sem("s_rzT")
        s_rx = sem("s_rx")
        s_rp = sem("s_rp")
        s_rpe = sem("s_rpe")
        s_rsg = sem("s_rsg")
        s_conv = sem("s_conv")
        s_rs = sem("s_rs")
        s_uf = sem("s_uf")
        s_u = sem("s_u")
        s_rg = sem("s_rg")
        s_ract = sem("s_ract")
        s_bu = sem("s_bu")
        s_scan = sem("s_scan")
        s_cy = sem("s_cy")
        s_ro = sem("s_ro")
        s_res = sem("s_res")
        s_x3 = sem("s_x3")
        s_zT3 = sem("s_zT3")
        s_xT3 = sem("s_xT3")
        s_lg3 = sem("s_lg3")
        s_fin = sem("s_fin")
        s_store = sem("s_store")

        MISC = [bank[6], bank[7]]
        SB_ = [bank[0], bank[1]]
        DA, PT = bank[2], bank[3]
        CTX = [bank[4], bank[5]]

        def uof(u):
            n, h = divmod(u, H)
            b, i = divmod(n, TB)
            g, j = divmod(h, HG)
            return b, i, h, g, j, n

        def bq_ready(b, g):
            return 2 * (NG * b + g) + 2

        block = ctx.enter_context(nc.Block())

        @block.sync
        def _(eng):
            eng.dma_start(xa[:, 0:TB, :], x_view[:, 0:TB, :]).then_inc(s_x[0], 16)
            eng.dma_start(ca[:, :], ca_in[:, :]).then_inc(s_ca, 16)
            eng.dma_start(ct, ct_in[:, :]).then_inc(s_ct, 16)
            eng.dma_start(xa[:, TB:, :], x_view[:, TB:, :]).then_inc(s_x[1], 16)
            eng.dma_start(cb[:, :], cb_in[:, :]).then_inc(s_cb, 16)
            eng.dma_start(wp0, wp0_in[:, :]).then_inc(s_w0, 16)
            eng.wait_ge(s_set, 4)
            for l, nt in ((0, NT0), (1, NT1)):
                for m in range(0, nt, 3):
                    eng.dma_start(xs[l][m * P:(m + 3) * P, :].rearrange("(t p) d -> p t d", p=P),
                                  zeros[:, 0:3 * D].rearrange("p (t d) -> p t d", t=3)).then_inc(s_zs, 16)

            def expert_rows(l, nt):
                def load(m, r):
                    eng.wait_ge(s_xT[l], m - RING + 1)
                    eng.dma_start(xt[:, r, :], xs[l][bass.ds(m * P, P), :]).then_inc(s_xload[l][r], 16)

                def store(m, r):
                    eng.wait_ge(s_yb[l], m + 1)
                    eng.dma_start(ys[l][bass.ds(m * P, P), :], yb[:, r, :]).then_inc(s_ystore[l][r], 16)

                eng.wait_ge(s_disp[l], 16 * NTOK)
                for r in range(RING):
                    eng.dma_start(xt[:, r, :], xs[l][r * P:(r + 1) * P, :]).then_inc(s_xload[l][r], 16)
                for m in range(2 * RING):
                    load(m + RING, m % RING)
                    if m >= 2:
                        store(m - 2, (m - 2) % RING)
                with eng.Fori(2, nt // RING - 1) as it:
                    for r in range(RING):
                        load(it * RING + (r + RING), r)
                        store(it * RING + (r - 2), (r - 2) % RING)
                for m in range(nt - RING - 2, nt):
                    store(m, m % RING)

            eng.wait_ge(s_out, len(jobs))
            eng.wait_ge(s_score, B * TB * H)
            eng.wait_ge(s_q, 2 * NG * B)
            eng.dma_start(wp1, wp1_in[:, :]).then_inc(s_w1, 16)
            expert_rows(0, NT0)
            expert_rows(1, NT1)
            for b in range(B):
                eng.wait_ge(s_fin, TB * (b + 1))
                eng.dma_start(out_view[:, b * TB:(b + 1) * TB, :], xc[:, b * TB:(b + 1) * TB, :]).then_inc(s_store, 16)
            eng.wait_ge(s_store, 16 * B)

        @block.gpsimd
        def _(eng):
            eng.memset(half[:, :], -0.5).then_inc(s_set, 1)
            eng.memset(qvT[:, :, S:QW], 0.0).then_inc(s_set, 1)
            eng.memset(qa[:, :, :, S:QW], 0.0).then_inc(s_set, 1)
            eng.memset(zeros[:, :], 0.0).then_inc(s_set, 1)
            eng.wait_ge(s_set, 4)
            steps = [0]

            def rsqrt(var, dst, width, scale, eps, need):
                eng.wait_ge(*need)
                if steps[0]:
                    eng.wait_ge(s_gstep, steps[0])
                eng.tensor_scalar(dst, var, scale, eps, ALU.mult, ALU.add).then_inc(s_gstep, 1)
                steps[0] += 1
                eng.wait_ge(s_gstep, steps[0])
                eng.tensor_tensor(dst, dst, half[:, 0:width], ALU.pow).then_inc(s_pow, 1)

            for e in plan:
                kind, b = e[0], e[1]
                if kind == "stats":
                    rsqrt(mv[:, 0, :, 1], rstd[:, 0, :], TB, 1.0, 1e-5, (s_var, variance[e]))
                    if b < 2:
                        eng.wait_ge(s_x[b], 16)
                    eng.tensor_tensor(xb[:, b * TB:(b + 1) * TB, :], xa[:, b * TB:(b + 1) * TB, :],
                                      A("bo").unsqueeze(1).broadcast_to([P, TB, D]), ALU.add).then_inc(s_xbo, 1)
                elif kind == "post":
                    rsqrt(mv[:, 1, :, 1], rstd[:, 1, :], TB, 1.0, 1e-5, (s_var, variance[e]))
                elif kind == "rms":
                    rsqrt(ssq[:, b * TB:(b + 1) * TB], rstd[:, 2, :], TB, 1.0 / D, 1e-6, (s_sq, TB * (b + 1)))
            nvar = len(variance)

            def move(l, rows_from, ready):
                eng.wait_ge(s_zs, 16 * ((NT0 + NT1) // 3))
                eng.wait_ge(*ready)
                for t in range(NTOK):
                    eng.indirect_dma_start(xs[l][:, :], bass.IndirectOffsetOnAxis(ap=pos[:, t:t + 1], axis=0),
                                           rows_from[:, t, :], None).then_inc(s_disp[l], 16)
                for r in range(RING):
                    eng.wait_ge(s_ystore[l][r], 16 * ((NT0, NT1)[l] // RING))
                for t in range(NTOK):
                    eng.indirect_dma_start(xa[:, t, :], None, ys[l][:, :],
                                           bass.IndirectOffsetOnAxis(ap=pos[:, t:t + 1], axis=0))\
                       .then_inc(s_gath[l][t // TB], 16)

            move(0, xc, (s_rt, 4))
            for b in range(B):
                nvar += 1
                rsqrt(mv[:, 1, :, 1], rstd[:, 1, :], TB, 1.0, 1e-5, (s_var, nvar))
            for kind, b in plan_recurrence():
                r = b % 2
                if kind == "P":
                    nvar += 1
                    rsqrt(mv[:, 0, :, 1], rstd[:, 0, :], TB, 1.0, 1e-5, (s_var, nvar))
                    for c in range(NC):
                        eng.wait_ge(s_uf, NC * b + c + 1)
                        eng.wait_ge(s_rsg, NC * b + c + 1)
                        eng.tensor_tensor(uu[:, r, c, :], uu[:, r, c, :], sg[:, r, c, :], ALU.mult).then_inc(s_u, 1)
                elif kind == "G":
                    for c in range(NC):
                        eng.wait_ge(s_ract, 3 * (NC * b + c) + 2)
                        eng.tensor_tensor(gb[:, r, c, :], gb[:, r, c, :], uu[:, r, c, :], ALU.mult).then_inc(s_bu, 1)
                    for c in range(NC):
                        eng.wait_ge(s_scan, NC * b + c + 1)
                        eng.wait_ge(s_ract, 3 * (NC * b + c) + 3)
                        eng.tensor_tensor(ga[:, r, c, :], ga[:, r, c, :], gc[:, r, c, :], ALU.mult).then_inc(s_cy, 1)
                        eng.wait_ge(s_cy, 2 * (NC * b + c) + 1)
                        eng.tensor_tensor(ga[:, r, c, :], ga[:, r, c, :], uu[:, r, c, :], ALU.add).then_inc(s_cy, 1)
                elif kind == "O":
                    nvar += 1
                    rsqrt(mv[:, 1, :, 1], rstd[:, 1, :], TB, 1.0, 1e-5, (s_var, nvar))
            move(1, xb, (s_rt, 8))
            for b in range(B):
                nvar += 1
                rsqrt(mv[:, 1, :, 1], rstd[:, 1, :], TB, 1.0, 1e-5, (s_var, nvar))

        @block.scalar
        def _(eng):
            for kind, *w in plan:
                if kind == "score":
                    u = w[0]
                    b, i, h, g, j, n = uof(u)
                    eng.wait_ge(s_fixed, u + 1)
                    if u >= 2:
                        eng.wait_ge(s_pT, u - 1)
                    if h == 0 and n >= 2:
                        eng.wait_ge(s_norm, n - 1)
                    eng.activation(prob[:, u % 2, :], SB_[u % 2][:, :], ACT.Exp, bias=nmax[:, u % 2, :],
                                   accum_out=rsum[:, n % 2, h:h + 1]).then_inc(s_exp, 1)
                elif kind == "probs":
                    u = w[0]
                    eng.wait_ge(s_pT, u + 1)
                    if u >= 2:
                        eng.wait_ge(s_pv, u - 1)
                    eng.activation(probT[:, u % 2, :], PT[:, :], ACT.Copy).then_inc(s_pTs, 1)
                elif kind == "rms":
                    b = w[0]
                    for t in range(b * TB, b * TB + TB):
                        eng.wait_ge(s_x1, t + 1)
                        if t:
                            eng.wait_ge(s_sq, t)
                        eng.activation(junk[:, :], xb[:, t, :], ACT.Square, accum_out=ssq[:, t:t + 1])\
                           .then_inc(s_sq, 1)

            def router_exp(l, E, need):
                eng.wait_ge(s_rt, need)
                eng.activation(rt[1][:, 0:NTOK * E], rt[0][:, 0:NTOK * E], ACT.Exp).then_inc(s_rte, 1)

            def experts(l, nt, F, func):
                CH = F // P

                def tile(m, r, first):
                    eng.wait_ge(s_h[l], m + 1)
                    if not first:
                        eng.wait_ge(s_y[l], m - (RING - 1))
                    for c in range(CH):
                        eng.activation(hT[:, r, c * P:(c + 1) * P], bank[r][:, c * P:(c + 1) * P], func,
                                       bias=wbuf[:, r, 2 * F + c:2 * F + c + 1]).then_inc(s_act[l], 1)

                for m in range(2 * RING):
                    tile(m, m % RING, m < RING)
                with eng.Fori(2, nt // RING) as it:
                    for r in range(RING):
                        tile(it * RING + r, r, False)

            router_exp(0, E0, 1)
            experts(0, NT0, F0, ACT.Silu)
            for kind, b in plan_recurrence():
                r = b % 2
                if kind == "P":
                    for c in range(NC):
                        eng.wait_ge(s_rp, 2 * NC * b + NC + c + 1)
                        if b >= 2:
                            eng.wait_ge(s_u, NC * (b - 2) + c + 1)
                        eng.activation(sg[:, r, c, :], bank[NC + c][:, :], ACT.Sigmoid, bias=C("bin", NC + c, 1))\
                           .then_inc(s_rsg, 1)
                    for c in range(NC):
                        eng.wait_ge(s_conv, NC * b + c + 1)
                        if b >= 1:
                            eng.wait_ge(s_uf, NC * (b - 1) + c + 1)
                        eng.activation(sc[:, c, :], cv[:, c, :], ACT.Sigmoid, bias=C("cb", c, 1)).then_inc(s_rs, 1)
                elif kind == "G":
                    for c in range(NC):
                        for q, (dst, f, bias) in enumerate(((ga, ACT.Sigmoid, "ba"), (gb, ACT.Sigmoid, "bb"),
                                                            (gc, ACT.Tanh, "bc"))):
                            eng.wait_ge(s_rg, 3 * (NC * b + c) + q + 1)
                            if b >= 2:
                                if q == 0:
                                    eng.wait_ge(s_ro, b - 1)
                                if q == 1:
                                    eng.wait_ge(s_scan, NC * (b - 2) + c + 1)
                                if q == 2:
                                    eng.wait_ge(s_cy, 2 * (NC * (b - 2) + c) + 1)
                            eng.activation(dst[:, r, c, :], bank[4 + (3 * (NC * b + c) + q) % 2][:, :], f,
                                           bias=C(bias, c, 1)).then_inc(s_ract, 1)
            router_exp(1, E1, 5)
            experts(1, NT1, F1, ACT.Gelu)

        @block.tensor
        def _(eng):
            ident = A("ident")
            eng.wait_ge(s_ca, 16)
            for kind, *w in plan:
                if kind == "score":
                    u = w[0]
                    b, i, h, g, j, n = uof(u)
                    rows = slice(32 * j, 32 * j + 32)
                    if u >= 2:
                        eng.wait_ge(s_exp, u - 1)
                    if u >= 1:
                        eng.wait_ge(s_diag, u)
                    if i == 0 and j == 0:
                        eng.wait_ge(s_q, bq_ready(b, g))
                    lhs = slice(i * P, (i + 1) * P)
                    r = b % 2
                    if i:
                        eng.matmul(SB_[u % 2][:, 0:i * P], qa[rows, r, g, lhs], ka[rows, r, g, 0:i * P],
                                   start=True, stop=True)
                    eng.matmul(SB_[u % 2][:, i * P:S], qb[rows, r, g, lhs], kb[rows, r, g, i * P:S],
                               start=True, stop=True)
                    eng.matmul(DA[:, 0:P], qa[rows, r, g, lhs], ka[rows, r, g, i * P:(i + 1) * P],
                               start=True, stop=True).then_inc(s_score, 1)
                elif kind == "probs":
                    u = w[0]
                    eng.wait_ge(s_exp, u + 1)
                    if u >= 1:
                        eng.wait_ge(s_pTs, u)
                    for t in range(TB):
                        mm = eng.transpose(PT[:, t * P:(t + 1) * P], prob[:, u % 2, t * P:(t + 1) * P], ident)
                    mm.then_inc(s_pT, 1)
                elif kind == "values":
                    u = w[0]
                    b, i, h, g, j, n = uof(u)
                    eng.wait_ge(s_pTs, u + 1)
                    if h == 0 and n >= 2:
                        eng.wait_ge(s_norm, n - 1)
                    for t in range(TB):
                        mm = eng.matmul(CTX[n % 2][:, h * DH:(h + 1) * DH], probT[:, u % 2, t * P:(t + 1) * P],
                                        vv[:, b % 2, t, h * DH:(h + 1) * DH], start=(t == 0), stop=(t == TB - 1))
                    mm.then_inc(s_pv, 1)
                elif kind == "job":
                    k = w[0]
                    name, *a = jobs[k]
                    bk = MISC[k % 2]
                    if k >= 2:
                        eng.wait_ge(s_out, k - 1)

                    def after(*other):
                        eng.wait_ge(s_out, number[other] + 1)

                    if name == "pem":
                        mm = eng.matmul(bk[:, 0:H], A("wp"), A("pem"), start=True, stop=True)
                    elif name == "zT":
                        eng.wait_ge(s_z, TB * (a[0] + 1))
                        for t in range(TB):
                            mm = eng.transpose(bk[:, t * P:(t + 1) * P], z[:, t, :], ident)
                    elif name == "q":
                        after("zT", a[0])
                        mm = eng.matmul(bk[:, :], A("wq"), xnT[:, :], start=True, stop=True)
                    elif name == "k":
                        after("zT", a[0])
                        mm = eng.matmul(bk[:, :], A(f"wk{a[1]}"), xnT[:, :], start=True, stop=True)
                    elif name == "v":
                        after("zT", a[0])
                        for t in range(TB):
                            mm = eng.matmul(bk[:, t * P:(t + 1) * P], xnT[:, t * P:(t + 1) * P], A("wv"),
                                            start=True, stop=True)
                    elif name in ("t1", "t2"):
                        after("q", a[0])
                        mm = eng.matmul(bk[:, :], A(f"m{name[1]}_{a[1]}"), qvT[:, a[0] % 2, 0:S], start=True, stop=True)
                    elif name == "corr":
                        after("q", a[0])
                        after("pem", 0)
                        eng.wait_ge(s_set, 4)
                        for t in range(TB):
                            mm = eng.matmul(bk[:, t * H:(t + 1) * H], qvT[:, a[0] % 2, t * P + 1:(t + 1) * P + 1],
                                            pm1[:, :], start=True, stop=True)
                    elif name == "ctxT":
                        eng.wait_ge(s_norm, a[0] + 1)
                        mm = eng.transpose(bk[:, 0:P], cn[:, :], ident)
                    elif name == "out":
                        after("ctxT", a[0])
                        mm = eng.matmul(bk[:, 0:D], cT[:, :], A("wo"), start=True, stop=True)
                    elif name == "xT":
                        eng.wait_ge(s_xn2, TB * (a[0] + 1))
                        for t in range(TB):
                            mm = eng.transpose(bk[:, t * P:(t + 1) * P], xc[:, a[0] * TB + t, :], ident)
                    elif name == "logits":
                        after("xT", a[0])
                        eng.wait_ge(s_cb, 16)
                        for t in range(TB):
                            mm = eng.matmul(bk[:, t * E0:(t + 1) * E0], xnT2[:, t * P:(t + 1) * P], C("gate"),
                                            start=True, stop=True)
                    mm.then_inc(s_job, 1)

            def counts(l, E):
                eng.wait_ge(s_rt, 4 * l + 2)
                eng.matmul(bank[0][:, 0:NTOK * E], C("upper"), rt[2][:, 0:NTOK * E], start=True, stop=True)\
                   .then_inc(s_rtp, 1)
                eng.matmul(bank[1][:, 0:NTOK * E], C("ones"), rt[2][:, 0:NTOK * E], start=True, stop=True)\
                   .then_inc(s_rtp, 1)

            def experts(l, nt, F):
                CH = F // P

                def transpose(m, r, it):
                    eng.wait_ge(s_xload[l][r], (it + 1) * 16)
                    if not (isinstance(m, int) and m == 0):
                        eng.wait_ge(s_xTs[l], m)
                    eng.transpose(bank[6][:, 0:P], xt[:, r, :], ident).then_inc(s_xT[l], 1)

                def hidden(m, r, first):
                    eng.wait_ge(s_xTs[l], m + 1)
                    eng.wait_ge(s_wb[l], m + 1)
                    if not first:
                        eng.wait_ge(s_act[l], (m - (RING - 1)) * CH)
                    for c in range(CH):
                        mm = eng.matmul(bank[r][:, c * P:(c + 1) * P], wbuf[:, r, c * P:(c + 1) * P], xTs[:, r, :],
                                        start=True, stop=True)
                    mm.then_inc(s_h[l], 1)

                def result(m, r, first):
                    eng.wait_ge(s_act[l], (m + 1) * CH)
                    if not first:
                        eng.wait_ge(s_yb[l], m - (RING - 1))
                    for c in range(CH):
                        mm = eng.matmul(bank[3 + r][:, 0:D], hT[:, r, c * P:(c + 1) * P],
                                        wbuf[:, r, F + c * D:F + (c + 1) * D], start=(c == 0), stop=(c == CH - 1))
                    mm.then_inc(s_y[l], 1)

                for m in range(2 * RING):
                    transpose(m, m % RING, m // RING)
                    if m >= 1:
                        hidden(m - 1, (m - 1) % RING, m - 1 < RING)
                    if m >= 2:
                        result(m - 2, (m - 2) % RING, m - 2 < RING)
                with eng.Fori(2, nt // RING) as it:
                    for r in range(RING):
                        transpose(it * RING + r, r, it)
                        hidden(it * RING + (r - 1), (r - 1) % RING, False)
                        result(it * RING + (r - 2), (r - 2) % RING, False)
                hidden(nt - 1, RING - 1, False)
                result(nt - 2, RING - 2, False)
                result(nt - 1, RING - 1, False)

            counts(0, E0)
            experts(0, NT0, F0)
            for kind, b in plan_recurrence():
                r = b % 2
                if kind == "P":
                    eng.wait_ge(s_z1, TB * (b + 1))
                    if b:
                        eng.wait_ge(s_rx, b)
                    for t in range(TB):
                        mm = eng.transpose(bank[6][:, t * P:(t + 1) * P], z[:, t, :], ident)
                    mm.then_inc(s_rzT, 1)
                    eng.wait_ge(s_rx, b + 1)
                    for c in range(2 * NC):
                        if b and c < NC:
                            eng.wait_ge(s_rpe, NC * (b - 1) + c + 1)
                        if b and c >= NC:
                            eng.wait_ge(s_rsg, NC * (b - 1) + c - NC + 1)
                        eng.matmul(bank[c][:, :], C("win", c * P, P), xnT[:, :], start=True, stop=True)\
                           .then_inc(s_rp, 1)
                elif kind == "G":
                    eng.wait_ge(s_u, NC * (b + 1))
                    for c in range(NC):
                        for q, name in enumerate(("wa", "wb", "wc")):
                            v = 3 * (NC * b + c) + q
                            if v >= 2:
                                eng.wait_ge(s_ract, v - 1)
                            for k in range(NC):
                                mm = eng.matmul(bank[4 + v % 2][:, :], C(name, k * INNER + c * P, P), uu[:, r, k, :],
                                                start=(k == 0), stop=(k == NC - 1))
                            mm.then_inc(s_rg, 1)
                else:
                    eng.wait_ge(s_cy, 2 * NC * (b + 1))
                    if b:
                        eng.wait_ge(s_res, TB * b)
                    for t in range(TB):
                        for k in range(NC):
                            mm = eng.matmul(bank[7][:, t * P:(t + 1) * P], ga[:, r, k, t * P:(t + 1) * P],
                                            C("wo1", k * D, D), start=(k == 0), stop=(k == NC - 1))
                    mm.then_inc(s_ro, 1)
            for b in range(B):
                eng.wait_ge(s_x3, TB * (b + 1))
                if b:
                    eng.wait_ge(s_xT3, b)
                for t in range(TB):
                    mm = eng.transpose(bank[6][:, t * P:(t + 1) * P], xb[:, b * TB + t, :], ident)
                mm.then_inc(s_zT3, 1)
                eng.wait_ge(s_xT3, b + 1)
                if b == 0:
                    eng.wait_ge(s_res, TB * B)
                for t in range(TB):
                    mm = eng.matmul(bank[7][:, (b * TB + t) * E1:(b * TB + t + 1) * E1], xnT[:, t * P:(t + 1) * P],
                                    C("router"), start=True, stop=True)
                mm.then_inc(s_lg3, 1)
            counts(1, E1)
            experts(1, NT1, F1)

        @block.vector
        def _(eng):
            last = [None]
            tally = {}

            def count(s):
                tally[s.name] = tally.get(s.name, 0) + 1
                last[0] = (s, tally[s.name])
                return s

            def own():
                eng.wait_ge(*last[0])

            eng.wait_ge(s_ca, 16)
            eng.tensor_tensor(col[:, 0:1], A("bq"), A("v"), ALU.add).then_inc(count(s_v), 1)
            for g in range(NG):
                eng.tensor_tensor(col[:, 1 + g:2 + g], A(f"u{g}"), A(f"v{g}"), ALU.subtract).then_inc(count(s_v), 1)

            def stats(rows, half_, sem_out):
                own()
                for t in range(TB):
                    eng.bn_stats(st[:, t, :], rows(t)).then_inc(count(s_v), 1)
                own()
                for t in range(TB):
                    eng.bn_aggr(mv[:, half_, t, :], st[:, t, :]).then_inc(count(sem_out if t == TB - 1 else s_v), 1)

            def normed(dst, rows, k, sem_each):
                own()
                for t in range(TB):
                    eng.tensor_scalar(dst(t), rows(t), mv[:, k, t, 0:1], rstd[:, k, t:t + 1], ALU.subtract, ALU.mult)\
                       .then_inc(count(sem_each), 1)

            for kind, *w in plan:
                if kind == "stats":
                    b = w[0]
                    if b < 2:
                        eng.wait_ge(s_x[b], 16)
                    stats(lambda t: xa[:, b * TB + t, :], 0, s_var)
                elif kind == "normz":
                    b = w[0]
                    if b:
                        eng.wait_ge(s_job, number[("zT", b - 1)] + 1)
                    eng.wait_ge(s_pow, power[("stats", b)])
                    normed(lambda t: z[:, t, :], lambda t: xa[:, b * TB + t, :], 0, s_z)
                elif kind == "score":
                    u = w[0]
                    b, i, h, g, j, n = uof(u)
                    sc_b = SB_[u % 2]
                    eng.wait_ge(s_score, u + 1)
                    eng.copy_predicated(sc_b[:, i * P:(i + 1) * P], A("tri").bitcast(U32), DA[:, 0:P])\
                       .then_inc(count(s_diag), 1)
                    own()
                    wide = min(P, S - 1 - i * P)
                    eng.scalar_tensor_tensor(out=sc_b[:, i * P + 1:i * P + 1 + wide], in0=A("ident")[:, 0:wide],
                                             scalar=corr[:, b % 2, i, h:h + 1],
                                             in1=sc_b[:, i * P + 1:i * P + 1 + wide],
                                             op0=ALU.mult, op1=ALU.add).then_inc(count(s_v), 1)
                    own()
                    if u >= 2:
                        eng.wait_ge(s_exp, u - 1)
                    eng.tensor_reduce(nmax[:, u % 2, :], sc_b[:, :], AX.X, ALU.max, negate=True)\
                       .then_inc(count(s_fixed), 1)
                elif kind == "norm":
                    n = w[0]
                    eng.wait_ge(s_exp, H * (n + 1))
                    own()
                    eng.reciprocal(rinv[:, :], rsum[:, n % 2, :]).then_inc(count(s_v), 1)
                    own()
                    eng.wait_ge(s_pv, H * (n + 1))
                    if n:
                        eng.wait_ge(s_job, number[("ctxT", n - 1)] + 1)
                    eng.tensor_tensor(cn[:, :].rearrange("p (h d) -> p h d", h=H),
                                      CTX[n % 2][:, 0:D].rearrange("p (h d) -> p h d", h=H),
                                      rinv[:, :].unsqueeze(2).broadcast_to([P, H, DH]), ALU.mult)\
                       .then_inc(count(s_norm), 1)
                elif kind == "post":
                    b = w[0]
                    stats(lambda t: xb[:, b * TB + t, :], 1, s_var)
                elif kind == "post2":
                    b = w[0]
                    eng.wait_ge(s_pow, power[("post", b)])
                    normed(lambda t: xb[:, b * TB + t, :], lambda t: xb[:, b * TB + t, :], 1, s_x1)
                elif kind == "job":
                    k = w[0]
                    name, *a = jobs[k]
                    bk = MISC[k % 2]
                    if name == "xT":
                        b = a[0]
                        eng.wait_ge(s_cb, 16)
                        eng.wait_ge(s_pow, power[("rms", b)])
                        for t in range(TB):
                            eng.scalar_tensor_tensor(out=xc[:, b * TB + t, :], in0=xb[:, b * TB + t, :],
                                                     scalar=rstd[:, 2, t:t + 1], in1=C("rms"),
                                                     op0=ALU.mult, op1=ALU.mult).then_inc(count(s_xn2), 1)
                    own()
                    eng.wait_ge(s_job, k + 1)
                    if name == "pem":
                        eng.tensor_copy(pm1[:, :], bk[:, 0:H]).then_inc(count(s_out), 1)
                    elif name == "zT":
                        if a[0]:
                            eng.wait_ge(s_job, number[("v", a[0] - 1)] + 1)
                        eng.tensor_scalar(xnT[:, :], bk[:, :], A("gamma"), A("beta"), ALU.mult, ALU.add)\
                           .then_inc(count(s_out), 1)
                    elif name == "q":
                        eng.tensor_scalar(qvT[:, a[0] % 2, 0:S], bk[:, :], col[:, 0:1], None, ALU.add)\
                           .then_inc(count(s_out), 1)
                    elif name == "k":
                        b, g = a
                        eng.wait_ge(s_ct, 16)
                        if b >= 2:
                            eng.wait_ge(s_score, (b - 1) * TB * H)
                        eng.scalar_tensor_tensor(out=ka[:, b % 2, g, :], in0=bk[:, :], scalar=A(f"bk{g}"),
                                                 in1=T(f"ka{g}"), op0=ALU.add, op1=ALU.add).then_inc(count(s_v), 1)
                        eng.scalar_tensor_tensor(out=kb[:, b % 2, g, :], in0=bk[:, :], scalar=A(f"bk{g}"),
                                                 in1=T(f"kb{g}"), op0=ALU.add, op1=ALU.add).then_inc(count(s_out), 1)
                    elif name == "v":
                        if a[0] >= 2:
                            eng.wait_ge(s_pv, (a[0] - 1) * TB * H)
                        eng.tensor_tensor(vv[:, a[0] % 2, :, :], bk[:, :].rearrange("p (t d) -> p t d", t=TB),
                                          A("bv").unsqueeze(1).broadcast_to([P, TB, D]), ALU.add)\
                           .then_inc(count(s_out), 1)
                    elif name == "t1":
                        eng.scalar_tensor_tensor(out=t1[:, :], in0=bk[:, :], scalar=col[:, 1 + a[1]:2 + a[1]],
                                                 in1=T(f"cos{a[1]}"), op0=ALU.add, op1=ALU.mult)\
                           .then_inc(count(s_out), 1)
                    elif name == "t2":
                        b, g = a
                        r = b % 2
                        eng.tensor_tensor(t2[:, :], bk[:, :], T(f"sin{g}"), ALU.mult).then_inc(count(s_out), 1)
                        own()
                        if b >= 2:
                            eng.wait_ge(s_score, (b - 1) * TB * H)
                        eng.wait_ge(s_set, 4)
                        eng.tensor_tensor(qa[:, r, g, 0:S], t1[:, :], t2[:, :], ALU.add).then_inc(count(s_q), 1)
                        own()
                        eng.tensor_scalar(t2[:, :], qa[:, r, g, 1:S + 1], A("pmask")[:, 0:1], None, ALU.mult)\
                           .then_inc(count(s_v), 1)
                        own()
                        eng.scalar_tensor_tensor(out=qb[:, r, g, :], in0=qa[:, r, g, 0:S], scalar=A("pmask")[:, 1:2],
                                                 in1=t2[:, :], op0=ALU.mult, op1=ALU.add).then_inc(count(s_q), 1)
                    elif name == "corr":
                        eng.tensor_copy(corr[:, a[0] % 2, :, :].rearrange("p t h -> p (t h)"), bk[:, 0:TB * H])\
                           .then_inc(count(s_out), 1)
                    elif name == "ctxT":
                        eng.tensor_copy(cT[:, :], bk[:, 0:P]).then_inc(count(s_out), 1)
                    elif name == "out":
                        eng.wait_ge(s_xbo, a[0] // TB + 1)
                        eng.tensor_tensor(xb[:, a[0], :], bk[:, 0:D], xb[:, a[0], :], ALU.add)\
                           .then_inc(count(s_out), 1)
                    elif name == "xT":
                        if a[0]:
                            eng.wait_ge(s_job, number[("logits", a[0] - 1)] + 1)
                        eng.tensor_copy(xnT2[:, :], bk[:, :]).then_inc(count(s_out), 1)
                    elif name == "logits":
                        b = a[0]
                        eng.tensor_copy(lg[:, b * TB * E0:(b + 1) * TB * E0], bk[:, 0:TB * E0])\
                           .then_inc(count(s_out), 1)

            def route(l, E, nt, width, logits):
                N = NTOK * E

                def ie(v):
                    return v[:, 0:N].rearrange("p (i e) -> p i e", e=E)

                def ei(v):
                    return v[:, 0:N].rearrange("p (e i) -> p i e", e=E)

                def over_e(v):
                    return v.unsqueeze(2).broadcast_to([P, NTOK, E])

                top, total, best, place = sm[:, 0, :], sm[:, 1, :], sm[:, 2, :], sm[:, 3, :]
                weight = sm[:, 4, :]
                ntile, upto = sm[:, 5, 0:E], sm[:, 0, 0:E]
                own()
                eng.tensor_reduce(top, ie(logits), AX.X, ALU.max).then_inc(count(s_v), 1)
                own()
                eng.tensor_tensor(ie(rt[0]), ie(logits), over_e(top), ALU.subtract).then_inc(count(s_rt), 1)
                own()
                eng.scalar_tensor_tensor(out=rt[3][:, 0:N], in0=rt[0][:, 0:N], scalar=0.0, in1=C(f"rev{l}"),
                                         op0=ALU.is_ge, op1=ALU.mult).then_inc(count(s_v), 1)
                own()
                eng.tensor_reduce(best, ie(rt[3]), AX.X, ALU.max).then_inc(count(s_v), 1)
                own()
                eng.tensor_tensor(ei(rt[2]), ie(rt[3]), over_e(best), ALU.is_equal).then_inc(count(s_rt), 1)
                eng.wait_ge(s_rte, l + 1)
                own()
                eng.tensor_reduce(total, ie(rt[1]), AX.X, ALU.add).then_inc(count(s_v), 1)
                own()
                eng.reciprocal(weight, total).then_inc(count(s_v), 1)
                eng.wait_ge(s_rtp, 2 * l + 2)
                own()
                eng.tensor_tensor_scan(rt[3][:, 0:N], C(f"run{l}"), bank[1][:, 0:N], 0.0, ALU.mult, ALU.add)\
                   .then_inc(count(s_v), 1)
                own()
                eng.tensor_tensor(rt[4][:, 0:N], rt[3][:, 0:N], bank[0][:, 0:N], ALU.add).then_inc(count(s_v), 1)
                own()
                eng.tensor_tensor(rt[4][:, 0:N], rt[4][:, 0:N], bank[1][:, 0:N], ALU.subtract).then_inc(count(s_v), 1)
                counts = rt[3][:, 0:N].rearrange("p (e i) -> p e i", e=E)[:, :, NTOK - 1:NTOK]
                eng.tensor_tensor(rt[1][:, 0:N].rearrange("p (e i) -> p e i", e=E),
                                  counts.broadcast_to([P, E, NTOK]),
                                  C(f"thr{l}").rearrange("p (e i) -> p e i", e=E), ALU.is_gt).then_inc(count(s_v), 1)
                own()
                eng.tensor_reduce(ntile, rt[1][:, 0:N].rearrange("p (e i) -> p e i", e=E), AX.X, ALU.add)\
                   .then_inc(count(s_v), 1)
                own()
                eng.tensor_tensor_scan(upto, C("ones", 0, E), ntile, 0.0, ALU.mult, ALU.add).then_inc(count(s_v), 1)
                own()
                ends = rt[1][0:1, 0:E * NTOK]
                M = nt * E
                eng.tensor_tensor(slotcmp[0:1, 0:M].rearrange("p (m e) -> p m e", e=E),
                                  sm[0:1, 0, 0:E].unsqueeze(1).broadcast_to([1, nt, E]),
                                  C(f"slot{l}", rows=slice(0, 1)).rearrange("p (m e) -> p m e", e=E), ALU.is_le)\
                   .then_inc(count(s_v), 1)
                own()
                eng.tensor_reduce(tex[:, 0:nt], slotcmp[0:1, 0:M].rearrange("p (m e) -> p m e", e=E), AX.X, ALU.add)\
                   .then_inc(count(s_v), 1)
                own()
                eng.tensor_scalar(offs[:, 0:nt], tex[:, 0:nt], float(E - 1), float(width), ALU.min, ALU.mult)\
                   .then_inc(count(s_rt), 1)
                eng.tensor_tensor(ntile, upto, ntile, ALU.subtract).then_inc(count(s_v), 1)
                own()
                eng.scalar_tensor_tensor(out=rt[3][:, 0:N].rearrange("p (e i) -> p e i", e=E),
                                         in0=ntile.unsqueeze(2).broadcast_to([P, E, NTOK]), scalar=float(P),
                                         in1=rt[4][:, 0:N].rearrange("p (e i) -> p e i", e=E),
                                         op0=ALU.mult, op1=ALU.add).then_inc(count(s_v), 1)
                own()
                eng.tensor_tensor(rt[4][:, 0:N], rt[3][:, 0:N], rt[2][:, 0:N], ALU.mult).then_inc(count(s_v), 1)
                own()
                eng.tensor_reduce(place, ei(rt[4]), AX.X, ALU.add).then_inc(count(s_v), 1)
                own()
                eng.tensor_copy(pos[:, :], place).then_inc(count(s_rt), 1)
                own()

            def experts(l, nt, F, width, wp):
                def fetch(m, r, first):
                    off = eng.value_load(offs[0:1, bass.ds(m, 1)], min_val=0, max_val=((E0, E1)[l] - 1) * width)
                    if not first:
                        eng.wait_ge(s_y[l], m - (RING - 1))
                        eng.wait_ge(s_yb[l], m - (RING - 1))
                    eng.tensor_copy(wbuf[:, r, 0:width], wp[:, bass.ds(off, width)]).then_inc(s_wb[l], 1)

                def turned(m, r, first):
                    eng.wait_ge(s_xT[l], m + 1)
                    if not first:
                        eng.wait_ge(s_h[l], m - (RING - 1))
                    eng.tensor_copy(xTs[:, r, :], bank[6][:, 0:P]).then_inc(s_xTs[l], 1)

                def result(m, r, turn, first):
                    eng.wait_ge(s_y[l], m + 1)
                    if not first:
                        eng.wait_ge(s_ystore[l][r], turn * 16)
                    eng.wait_ge(s_wb[l], m + 1)
                    eng.tensor_tensor(yb[:, r, :], bank[3 + r][:, 0:D], wbuf[:, r, 2 * F + F // P:width], ALU.add)\
                       .then_inc(s_yb[l], 1)

                eng.wait_ge(*((s_w0, 16), (s_w1, 16))[l])
                for m in range(2 * RING):
                    fetch(m, m % RING, m < RING)
                    turned(m, m % RING, m < RING)
                    if m >= 2:
                        result(m - 2, (m - 2) % RING, (m - 2) // RING, m - 2 < RING)
                with eng.Fori(2, nt // RING) as it:
                    for r in range(RING):
                        fetch(it * RING + r, r, False)
                        turned(it * RING + r, r, False)
                        result(it * RING + (r - 2), (r - 2) % RING, it if r == 2 else it - 1, False)
                for m in range(nt - 2, nt):
                    result(m, m % RING, m // RING, False)
                last[0] = (s_yb[l], nt)

            def after_experts(l, b, dst, sem_each):
                eng.wait_ge(s_gath[l][b], 16 * TB)
                base = (xb, xb)[l]
                own()
                for t in range(b * TB, (b + 1) * TB):
                    eng.scalar_tensor_tensor(out=dst[:, t, :], in0=xa[:, t, :], scalar=sm[:, 4, t:t + 1],
                                             in1=base[:, t, :], op0=ALU.mult, op1=ALU.add).then_inc(count(s_v), 1)
                stats(lambda t: dst[:, b * TB + t, :], 1, s_var)
                nvar[0] += 1
                npow[0] += 1
                eng.wait_ge(s_pow, npow[0])
                normed(lambda t: dst[:, b * TB + t, :], lambda t: dst[:, b * TB + t, :], 1, sem_each)

            nvar, npow = [len(variance)], [len(power)]
            route(0, E0, NT0, WW0, lg)
            experts(0, NT0, F0, WW0, wp0)
            for t in range(B):
                after_experts(0, t, xc, s_v)
            for r in range(2):
                for c in range(NC):
                    own()
                    eng.memset(pj[:, r, c, 0:2], 0.0).then_inc(count(s_v), 1)
            for kind, b in plan_recurrence():
                r = b % 2
                if kind == "P":
                    stats(lambda t: xc[:, b * TB + t, :], 0, s_var)
                    npow[0] += 1
                    eng.wait_ge(s_pow, npow[0])
                    if b:
                        eng.wait_ge(s_rzT, b)
                    normed(lambda t: z[:, t, :], lambda t: xc[:, b * TB + t, :], 0, s_z1)
                    eng.wait_ge(s_rzT, b + 1)
                    if b:
                        eng.wait_ge(s_rp, 2 * NC * b)
                    eng.tensor_scalar(xnT[:, :], bank[6][:, :], C("gamma1"), C("beta1"), ALU.mult, ALU.add)\
                       .then_inc(count(s_rx), 1)
                    for c in range(NC):
                        eng.wait_ge(s_rp, 2 * NC * b + c + 1)
                        own()
                        eng.tensor_scalar(pj[:, r, c, 2:2 + S], bank[c][:, :], C("bin", c, 1), None, ALU.add)\
                           .then_inc(count(s_rpe), 1)
                    for c in range(NC):
                        if b:
                            eng.wait_ge(s_rs, NC * (b - 1) + c + 1)
                        own()
                        eng.tensor_scalar(cv[:, c, :], pj[:, r, c, 0:S], C("cw", 3 * c, 1), None, ALU.mult)\
                           .then_inc(count(s_v), 1)
                        for k in (1, 2):
                            own()
                            eng.scalar_tensor_tensor(out=cv[:, c, :], in0=pj[:, r, c, k:k + S],
                                                     scalar=C("cw", 3 * c + k, 1), in1=cv[:, c, :],
                                                     op0=ALU.mult, op1=ALU.add)\
                               .then_inc(count(s_conv if k == 2 else s_v), 1)
                    for c in range(NC):
                        eng.wait_ge(s_rs, NC * b + c + 1)
                        if b >= 2:
                            eng.wait_ge(s_cy, 2 * NC * (b - 1))
                            eng.wait_ge(s_rg, 3 * NC * (b - 1))
                        own()
                        eng.scalar_tensor_tensor(out=uu[:, r, c, :], in0=cv[:, c, :], scalar=C("cb", c, 1),
                                                 in1=sc[:, c, :], op0=ALU.add, op1=ALU.mult).then_inc(count(s_uf), 1)
                elif kind == "G":
                    for c in range(NC):
                        eng.wait_ge(s_bu, NC * b + c + 1)
                        own()
                        eng.tensor_tensor_scan(ga[:, r, c, :], ga[:, r, c, :], gb[:, r, c, :], 0.0, ALU.mult, ALU.add)\
                           .then_inc(count(s_scan), 1)
                else:
                    eng.wait_ge(s_ro, b + 1)
                    own()
                    for t in range(TB):
                        n = b * TB + t
                        eng.scalar_tensor_tensor(out=xb[:, n, :], in0=xc[:, n, :], scalar=2.0,
                                                 in1=bank[7][:, t * P:(t + 1) * P], op0=ALU.mult, op1=ALU.add)\
                           .then_inc(count(s_res), 1)
                    own()
                    for t in range(TB):
                        n = b * TB + t
                        eng.tensor_tensor(xb[:, n, :], xb[:, n, :], C("bo1"), ALU.add).then_inc(count(s_v), 1)
                    stats(lambda t: xb[:, b * TB + t, :], 1, s_var)
                    npow[0] += 1
                    eng.wait_ge(s_pow, npow[0])
                    normed(lambda t: xb[:, b * TB + t, :], lambda t: xb[:, b * TB + t, :], 1, s_x3)
            for b in range(B):
                eng.wait_ge(s_zT3, b + 1)
                eng.wait_ge(s_rp, 2 * NC * B)
                if b:
                    eng.wait_ge(s_lg3, b)
                own()
                eng.tensor_copy(xnT[:, :], bank[6][:, :]).then_inc(count(s_xT3), 1)
            eng.wait_ge(s_lg3, B)
            own()
            eng.tensor_copy(lg[:, 0:NTOK * E1], bank[7][:, 0:NTOK * E1]).then_inc(count(s_v), 1)
            route(1, E1, NT1, WW1, lg)
            experts(1, NT1, F1, WW1, wp1)
            for b in range(B):
                after_experts(1, b, xc, s_fin)


def kernel(**inputs):
    import concourse.bacc as bacc
    from concourse.bass_utils import run_bass_kernel_spmd

    a = {k: np.asarray(v) for k, v in inputs.items()}
    f32 = np.float32
    eye = np.eye(P, dtype=f32)
    div = np.exp(np.arange(0, D, 2, dtype=f32) * f32(-np.log(10000.0) / D)).astype(np.float64)
    k = np.arange(S, dtype=np.float64)

    def diagonal(w, transposed=False):
        m = np.zeros((P, P), f32)
        for h in range(H):
            m[h * DH:(h + 1) * DH, h * DH:(h + 1) * DH] = w.T if transposed else w
        return m

    def column(v):
        return np.reshape(v, (-1, 1))

    def across(v):
        return np.broadcast_to(np.reshape(v, (1, -1)), (P, v.size))

    fa = {"ident": eye, "tri": np.tril(np.ones((P, P), f32)), "wq": diagonal(a["L0_attn_Wq"]),
          "wv": diagonal(a["L0_attn_Wv"]), "wp": diagonal(a["L0_attn_Wp"]),
          "gamma": column(a["L0_attn_ln_gamma"]), "beta": column(a["L0_attn_ln_beta"]),
          "bq": column(np.tile(a["L0_attn_bq"], H)), "v": column(a["L0_attn_v_bias"]),
          "bv": across(np.tile(a["L0_attn_bv"], H)), "bo": across(a["L0_attn_bo"]), "wo": a["L0_attn_Wo"]}
    ft = {}
    pem, pmask = np.zeros((P, H), f32), np.zeros((P, 2), f32)
    for h in range(H):
        w = div[h * DH // 2:(h + 1) * DH // 2]
        pem[h * DH:(h + 1) * DH:2, h] = SCALE * np.sin(w)
        pem[h * DH + 1:(h + 1) * DH:2, h] = -SCALE * np.cos(w)
    for g in range(NG):
        wk, m1, m2 = (np.zeros((P, P), f32) for _ in range(3))
        cols = {n: np.zeros((P, 1), f32) for n in ("bk", "u", "v")}
        cos, sin, ka, kb = np.full((P, S), SCALE, f32), np.zeros((P, S), f32), np.zeros((P, S), f32), np.zeros((P, S), f32)
        for j in range(HG):
            h = g * HG + j
            src, con, posn = slice(h * DH, (h + 1) * DH), slice(32 * j, 32 * j + DH), slice(32 * j + DH, 32 * j + 2 * DH)
            wk[src, con] = a["L0_attn_Wk"]
            m1[src, con] = np.eye(DH)
            m1[src, posn] = a["L0_attn_Wp"].T
            m2[src, posn] = a["L0_attn_Wp"].reshape(DH // 2, 2, DH)[:, ::-1].reshape(DH, DH).T
            cols["bk"][con, 0] = a["L0_attn_bk"]
            cols["u"][con, 0] = a["L0_attn_u_bias"][h]
            cols["v"][con, 0] = a["L0_attn_v_bias"][h]
            w = div[h * DH // 2:(h + 1) * DH // 2, None]
            s0, c0 = posn.start, posn.start + 1
            cos[s0:posn.stop:2] = SCALE * np.cos(w * k)
            cos[c0:posn.stop:2] = SCALE * np.cos(w * k)
            sin[s0:posn.stop:2] = SCALE * np.sin(w * k)
            sin[c0:posn.stop:2] = -SCALE * np.sin(w * k)
            for table, shift in ((ka, S - 1), (kb, -1)):
                table[s0:posn.stop:2] = np.sin(w * (k + shift))
                table[c0:posn.stop:2] = np.cos(w * (k + shift))
            pmask[posn, 0] = 1.0
            pmask[con, 1] = 1.0
        fa |= {f"wk{g}": wk, f"m1_{g}": m1, f"m2_{g}": m2, f"bk{g}": cols["bk"], f"u{g}": cols["u"], f"v{g}": cols["v"]}
        ft |= {f"cos{g}": cos, f"sin{g}": sin, f"ka{g}": ka, f"kb{g}": kb}
    fa |= {"pem": pem, "pmask": pmask}

    def chunks(w, n):
        return w.reshape(n, P, -1).transpose(1, 0, 2).reshape(P, -1)

    fb = {"upper": np.triu(np.ones((P, P), f32), 1), "ones": np.ones((P, P), f32), "rms": across(a["L0_ffn_rms_w"]),
          "gate": a["L0_ffn_gate_w"].T, "router": a["L1_ffn_router_w"], "bo1": across(a["L1_attn_bo"]),
          "gamma1": column(a["L1_attn_gamma"]), "beta1": column(a["L1_attn_beta"]), "win": a["L1_attn_W_in"],
          "bin": a["L1_attn_b_in"].reshape(2 * NC, P).T, "cw": chunks(a["L1_attn_conv_w"].reshape(INNER, 3), NC),
          "cb": a["L1_attn_conv_b"].reshape(NC, P).T, "wo1": chunks(a["L1_attn_Wo"], NC)}
    for n in "abc":
        fb["w" + n] = chunks(a["L1_attn_W" + n], NC)
        fb["b" + n] = a["L1_attn_b" + n].reshape(NC, P).T
    for l, (E, nt) in enumerate(((E0, NT0), (E1, NT1))):
        fb[f"rev{l}"] = across(np.tile(np.arange(E, 0, -1), NTOK))
        fb[f"run{l}"] = across(np.tile(np.arange(NTOK) > 0, E))
        fb[f"thr{l}"] = across(np.tile(P * np.arange(NTOK), E))
        fb[f"slot{l}"] = across(np.repeat(np.arange(nt), E))

    def packed(fields, values):
        return np.concatenate([np.asarray(values[n], f32).reshape(P, w) for n, w in fields], axis=1)

    def experts(w1, b1, w2, b2):
        E, _, F = w1.shape
        return np.concatenate([w1.transpose(1, 0, 2), w2.reshape(E, F // P, P, D).transpose(2, 0, 1, 3).reshape(P, E, -1),
                               b1.reshape(E, F // P, P).transpose(2, 0, 1), np.broadcast_to(b2[None], (P, E, D))],
                              axis=2).reshape(P, -1)

    arrays = {"x": a["L0_attn_inputs"], "ca": packed(FIELDS_A, fa), "ct": packed(FIELDS_T, ft), "cb": packed(FIELDS_B, fb),
              "wp0": experts(*(a["L0_ffn_" + n] for n in ("W1", "b1", "W2", "b2"))),
              "wp1": experts(*(a["L1_ffn_" + n] for n in ("w1", "b1", "w2", "b2")))}
    arrays = {n: np.ascontiguousarray(v) for n, v in arrays.items()}
    nc = bacc.Bacc("TRN2", target_bir_lowering=False, num_devices=1)
    args = [nc.dram_tensor(n + "_in", v.shape, F32, kind="ExternalInput").ap() for n, v in arrays.items()]
    args.append(nc.dram_tensor("out", (B, S, D), F32, kind="ExternalOutput").ap())
    build(nc, *args)
    r = run_bass_kernel_spmd(nc, [{n + "_in": v for n, v in arrays.items()}], core_ids=[0])
    return r.results[0]["out"]
```

```python
from contextlib import ExitStack

import numpy as np

import concourse.bass as bass
from concourse import mybir
from concourse.alu_op_type import AluOpType as ALU

F32 = mybir.dt.float32
I32 = mybir.dt.int32
U32 = mybir.dt.uint32
ACT = mybir.ActivationFunctionType
AX = mybir.AxisListType

P = 128
B, S, D = 4, 512, 128
TB = S // P
NTOK = B * TB
H, DH = 8, 16
HG = 4
NG = H // HG
SCALE = float(D) ** -0.5
E0, F0 = 8, 512
E1, F1 = 14, 256
INNER = 256
NC = INNER // P
RING = 3
AHEAD = 3
HP = 32


def slot_tiles(experts):
    most = (B * S + experts * (P - 1)) // P
    return -(-most // RING) * RING


NT0, NT1 = slot_tiles(E0), slot_tiles(E1)
WW0 = F0 + F0 + F0 // P + D
WW1 = F1 + F1 + F1 // P + D


def columns(fields):
    at, out = 0, {}
    for name, width in fields:
        out[name] = (at, width)
        at += width
    return out, at


FIELDS_A = [("ident", P), ("tri", P), ("wq", P), ("wk0", P), ("wk1", P), ("wv", 2 * P), ("m1_0", P), ("m1_1", P),
            ("m2_0", P), ("m2_1", P), ("wp", P), ("pem", H), ("gamma", 1), ("beta", 1), ("bq", 1), ("v", 1), ("pmask", 2),
            ("bk0", 1), ("bk1", 1), ("u0", 1), ("u1", 1), ("v0", 1), ("v1", 1), ("bv", 2 * D), ("bo", D),
            ("wo0", D), ("wo1", D)]
FIELDS_T = [("cos0", S), ("cos1", S), ("sin0", S), ("sin1", S), ("ka0", S), ("ka1", S), ("kb0", S), ("kb1", S)]
FIELDS_B = [("upper", P), ("ones", P), ("rms", D), ("gate", E0), ("router", E1), ("bo1", D),
            ("rev0", NTOK * E0), ("rev1", NTOK * E1), ("run0", NTOK * E0), ("run1", NTOK * E1),
            ("thr0", NTOK * E0), ("thr1", NTOK * E1), ("slot0", NT0 * E0), ("slot1", NT1 * E1),
            ("gamma1", 1), ("beta1", 1), ("win", 2 * INNER), ("bin", 2 * NC), ("cw", NC * 3), ("cb", NC),
            ("wa", NC * INNER), ("wb", NC * INNER), ("wc", NC * INNER), ("ba", NC), ("bb", NC), ("bc", NC),
            ("wo1", NC * D)]
COL_A, WIDE_A = columns(FIELDS_A)
COL_T, WIDE_T = columns(FIELDS_T)
COL_B, WIDE_B = columns(FIELDS_B)


def plan_attention():
    jobs, plan = [], []

    def job(name, *where):
        jobs.append((name, *where))
        plan.append(("job", len(jobs) - 1))

    def put(event):
        if event[0] == "job":
            job(*event[1:])
        else:
            plan.append(event)

    def projections(b):
        return [(2, ("stats", b)), (4, ("normz", b)), (6, ("job", "zT", b)), (8, ("job", "q", b)),
                (10, ("job", "k", b, 0)), (12, ("job", "k", b, 1)), (14, ("job", "v", b, 0)), (16, ("job", "v", b, 1)),
                (18, ("job", "t1", b, 0)), (20, ("job", "t2", b, 0)), (22, ("job", "corr", b)),
                (34, ("job", "t1", b, 1)), (36, ("job", "t2", b, 1))]

    waiting = {}
    per = TB * H
    put(("job", "pem", 0))
    for at, e in projections(0):
        if at < per:
            put(e)
        else:
            waiting.setdefault(at - per, []).append(e)
    units = B * TB * H
    for b in range(1, B):
        for at, e in projections(b):
            waiting.setdefault((b - 1) * per + at, []).append(e)
    for m in range(B * NG * TB):
        b, g, i = m // (NG * TB), m // TB % NG, m % TB
        at = HG * (m + 1)
        waiting.setdefault(at, []).append(("recip", m))
        waiting.setdefault(at + 1, []).append(("job", "rT", m))
        waiting.setdefault(at + 2, []).append(("norm", m))
        if g == NG - 1:
            waiting.setdefault(at + 3, []).append(("job", "out", b * TB + i))
            if i == TB - 1:
                waiting.setdefault(at + 5, []).append(("post", b))
                waiting.setdefault(at + 8, []).append(("post2", b))
                waiting.setdefault(at + 11, []).append(("rms", b))
                waiting.setdefault(at + 12, []).append(("job", "xT", b))
                waiting.setdefault(at + 14, []).append(("job", "logits", b))
    for u in range(AHEAD):
        plan.append(("score", u))
    for u in range(units + 16):
        if u < units:
            plan.append(("probs", u))
        if u + AHEAD < units:
            plan.append(("score", u + AHEAD))
        for e in waiting.pop(u, []):
            put(e)
        if 1 <= u <= units:
            plan.append(("values", u - 1))
    assert not waiting, waiting
    return jobs, plan


def plan_after_experts(l, steps_of=lambda b: [("normed", b)]):
    plan = [("gather", 0), ("gather", 1), ("sum", 0)]
    for b in range(1, B + 1):
        if b + 1 < B:
            plan.append(("gather", b + 1))
        if b < B:
            plan.append(("sum", b))
        plan += steps_of(b - 1)
    return plan


def plan_recurrence():
    head = {0: [("normed", 0)], 1: [("z", 0), ("in", 0), ("normed", 1)],
            2: [("conv", 0), ("normed", 2)], 3: [("normed", 3)]}
    plan = plan_after_experts(0, lambda b: head[b])
    for b in range(B + 1):
        if b + 1 < B:
            plan += [("z", b + 1), ("in", b + 1)]
        if b < B:
            plan += [("u", b)]
        if b >= 1:
            plan += [("out", b - 1)]
        if b < B:
            plan += [("gate", b)]
        if b + 1 < B:
            plan += [("conv", b + 1)]
        if b >= 1:
            plan += [("x3", b - 1), ("router", b - 1)]
        if b < B:
            plan += [("scan", b)]
        if b >= 1:
            plan += [("logits", b - 1)]
    return plan


def build(nc, x_in, ca_in, ct_in, cb_in, wp0_in, wp1_in, out):
    jobs, plan = plan_attention()
    number = {j: k for k, j in enumerate(jobs)}
    power = {e: k + 1 for k, e in enumerate(e for e in plan if e[0] in ("stats", "post", "rms"))}
    variance = {e: k + 1 for k, e in enumerate(e for e in plan if e[0] in ("stats", "post"))}

    middle = plan_recurrence()
    final = plan_after_experts(1)
    order = [(0, *e) for e in middle if e[0] in ("sum", "normed", "out")]
    order += [(1, *e) for e in final if e[0] == "sum"]
    place_of = {e: k + 1 for k, e in enumerate(order)}
    turn = {e: k + 1 for k, e in enumerate(e for e in middle if e[0] in ("in", "router", "logits"))}

    xs = [nc.dram_tensor(f"slots_in_{l}", (n * P, D), F32, kind="Internal").ap() for l, n in ((0, NT0), (1, NT1))]
    ys = [nc.dram_tensor(f"slots_out_{l}", (n * P, D), F32, kind="Internal").ap() for l, n in ((0, NT0), (1, NT1))]
    x_view = x_in.rearrange("b (t p) d -> p (b t) d", p=P)
    out_view = out.rearrange("b (t p) d -> p (b t) d", p=P)

    with ExitStack() as ctx:
        def sb(name, shape, dt=F32):
            return ctx.enter_context(nc.sbuf_tensor(name, shape, dt))

        def sem(name):
            return ctx.enter_context(nc.semaphore(name))

        bank = [ctx.enter_context(nc.psum_tensor(f"bank{i}", [P, 512], F32)) for i in range(8)]

        ca = sb("ca", [P, WIDE_A])
        cb = sb("cb", [P, WIDE_B])

        def A(name, rows=slice(None)):
            at, w = COL_A[name]
            return ca[rows, at:at + w]

        def C(name, a=0, n=None, rows=slice(None)):
            at, w = COL_B[name]
            return cb[rows, at + a:at + a + (w - a if n is None else n)]

        QW = S + 1
        WW = max(WW0, WW1)
        arena1 = sb("arena1", [P, max(WIDE_T + 2 * H * S + 4 * NG * S + QW, E1 * WW1 + RING * WW)])
        ct = arena1[:, 0:WIDE_T]
        at = WIDE_T
        qa = arena1[:, at:at + H * S].rearrange("p (h q) -> p h q", h=H)
        qb = arena1[:, at + H * S:at + 2 * H * S].rearrange("p (h q) -> p h q", h=H)
        at += 2 * H * S
        ka = arena1[:, at:at + 2 * NG * S].rearrange("p (r g q) -> p r g q", r=2, g=NG)
        kb = arena1[:, at + 2 * NG * S:at + 4 * NG * S].rearrange("p (r g q) -> p r g q", r=2, g=NG)
        at += 4 * NG * S
        qg = arena1[:, at:at + QW]
        wp1 = arena1[:, 0:E1 * WW1]
        wbuf = arena1[:, E1 * WW1:E1 * WW1 + RING * WW].rearrange("p (r w) -> p r w", r=RING)

        def T(name):
            at, w = COL_T[name]
            return ct[:, at:at + w]

        PJ = S + 2
        REC = NC * (2 * PJ + 5 * S * 2 + 2 * S)
        arena2 = sb("arena2", [P, max(E0 * WW0, REC)])
        wp0 = arena2[:, 0:E0 * WW0]
        att = arena2[:, E0 * WW0:REC]

        xa = sb("xa", [P, NTOK, D])
        xb = sb("xb", [P, NTOK, D])
        xc = sb("xc", [P, NTOK, D])
        z = sb("z", [P, TB, D])
        xnT = sb("xnT", [P, S])
        qvT = sb("qvT", [P, 2, QW])
        vv = att[:, 0:2 * TB * H * HP].rearrange("p (r t d) -> p r t d", r=2, t=TB)
        beside = 2 * TB * H * HP
        corr = sb("corr", [P, 2, TB, H])
        t1 = sb("t1", [P, S])
        t2 = sb("t2", [P, S])
        work = sb("work", [P, (AHEAD + 2) * S])
        prob = work[:, 0:AHEAD * S].rearrange("p (r k) -> p r k", r=AHEAD)
        probT = work[:, AHEAD * S:(AHEAD + 2) * S].rearrange("p (r k) -> p r k", r=2)
        hT = work[:, 0:RING * F0].rearrange("p (r f) -> p r f", r=RING)
        yb = work[:, RING * F0:RING * (F0 + D)].rearrange("p (r d) -> p r d", r=RING)
        cx = att[:, beside:beside + TB * NG * P].rearrange("p (i g q) -> p i g q", i=TB, g=NG)
        beside += TB * NG * P
        rT = att[:, beside:beside + P]
        rinv = att[:, beside + P:beside + 2 * P]
        rone = att[:, beside + 2 * P:beside + 2 * P + HG]
        col = sb("col", [P, 8])
        pm1 = sb("pm1", [P, H])
        nmax = sb("nmax", [P, AHEAD, 1])
        rsum = sb("rsum", [P, 3, HG])
        st = sb("st", [P, TB, 6])
        mv = sb("mv", [P, 2, TB, 2])
        rstd = sb("rstd", [P, 3, TB])
        sta = sb("sta", [P, NTOK, 6])
        mva = sb("mva", [P, 2, NTOK, 2])
        rstda = sb("rstda", [P, 2, NTOK])
        half = sb("half", [P, NTOK])
        junk = sb("junk", [P, D])
        xnT2 = sb("xnT2", [P, S])
        slotcmp = t1[0:1, :]
        ssq = sb("ssq", [P, NTOK])
        zeros = sb("zeros", [P, 512])
        lg = sb("lg", [P, NTOK * E1])
        rt = [sb(f"rt{i}", [P, NTOK * E1]) for i in range(5)]
        sm = sb("sm", [P, 6, NTOK])
        pos = sb("pos", [P, NTOK], I32)
        tex = sb("tex", [1, NT1])
        offs = sb("offs", [1, NT1], I32)
        xt = sb("xt", [P, RING, D])
        xTs = t2[:, 0:RING * P].rearrange("p (r q) -> p r q", r=RING)

        rec_at = [0]

        def rec(*dims):
            n = int(np.prod(dims))
            v = arena2[:, rec_at[0]:rec_at[0] + n]
            rec_at[0] += n
            names = "abc"[:len(dims)]
            return v.rearrange(f"p ({' '.join(names)}) -> p {' '.join(names)}", **{k: d for k, d in zip(names, dims)})

        pj = rec(2, NC, PJ)
        sg = rec(2, NC, S)
        uu = rec(2, NC, S)
        ga = rec(2, NC, S)
        gb = rec(2, NC, S)
        gc = rec(2, NC, S)
        cv = rec(NC, S)
        sc = rec(NC, S)
        assert rec_at[0] <= REC

        s_x = [sem(f"s_xin{k}") for k in range(2)]
        s_ca = sem("s_ca")
        s_ct = sem("s_ct")
        s_cb = sem("s_cb")
        s_w0 = sem("s_w0")
        s_w1 = sem("s_w1")
        s_zs = sem("s_zs")
        s_z = sem("s_z")
        s_x1 = sem("s_x1")
        s_xn2 = sem("s_xn2")
        s_xbo = sem("s_xbo")
        s_set = sem("s_set")
        s_pow = sem("s_pow")
        s_gstep = sem("s_gstep")
        s_v = sem("s_v")
        s_score = sem("s_score")
        s_fixed = sem("s_fixed")
        s_diag = sem("s_diag")
        s_exp = sem("s_exp")
        s_pT = sem("s_pT")
        s_pTs = sem("s_pTs")
        s_pv = sem("s_pv")
        s_job = sem("s_job")
        s_out = sem("s_out")
        s_qg = sem("s_qg")
        s_qa = sem("s_qa")
        s_qb = sem("s_qb")
        s_qz = sem("s_qz")
        s_rinv = sem("s_rinv")
        s_norm = sem("s_norm")
        s_var = sem("s_var")
        s_sq = sem("s_sq")
        s_rt = sem("s_rt")
        s_rte = sem("s_rte")
        s_rtp = sem("s_rtp")
        s_disp = [sem(f"s_disp{l}") for l in range(2)]
        s_gath = [[sem(f"s_gath{l}_{b}") for b in range(B)] for l in range(2)]
        s_xload = [[sem(f"s_xload{l}_{r}") for r in range(RING)] for l in range(2)]
        s_ystore = [[sem(f"s_ystore{l}_{r}") for r in range(RING)] for l in range(2)]
        s_xT = [sem(f"s_xT{l}") for l in range(2)]
        s_xTs = [sem(f"s_xTs{l}") for l in range(2)]
        s_wb = [sem(f"s_wb{l}") for l in range(2)]
        s_h = [sem(f"s_h{l}") for l in range(2)]
        s_act = [sem(f"s_act{l}") for l in range(2)]
        s_y = [sem(f"s_y{l}") for l in range(2)]
        s_yb = [sem(f"s_yb{l}") for l in range(2)]
        s_z1 = sem("s_z1")
        s_turn = sem("s_turn")
        s_took = sem("s_took")
        s_rp = sem("s_rp")
        s_rpe = sem("s_rpe")
        s_rsg = sem("s_rsg")
        s_conv = sem("s_conv")
        s_rs = sem("s_rs")
        s_uf = sem("s_uf")
        s_u = sem("s_u")
        s_rg = sem("s_rg")
        s_ract = sem("s_ract")
        s_bu = sem("s_bu")
        s_scan = sem("s_scan")
        s_cy = sem("s_cy")
        s_ro = sem("s_ro")
        s_res = sem("s_res")
        s_x3 = sem("s_x3")
        s_fin = sem("s_fin")
        s_store = sem("s_store")

        SCORE = bank[0:AHEAD]
        DA, PT = bank[3], bank[4]
        CTX = bank[5:7]
        JOB = bank[7]

        def uof(u):
            m, j = divmod(u, HG)
            b, g, i = m // (NG * TB), m // TB % NG, m % TB
            return b, i, g * HG + j, g, j, m

        block = ctx.enter_context(nc.Block())

        @block.sync
        def _(eng):
            eng.dma_start(xa[:, 0:TB, :], x_view[:, 0:TB, :]).then_inc(s_x[0], 16)
            eng.dma_start(ca[:, :], ca_in[:, :]).then_inc(s_ca, 16)
            eng.dma_start(ct, ct_in[:, :]).then_inc(s_ct, 16)
            eng.dma_start(xa[:, TB:, :], x_view[:, TB:, :]).then_inc(s_x[1], 16)
            eng.dma_start(cb[:, :], cb_in[:, :]).then_inc(s_cb, 16)
            eng.dma_start(wp0, wp0_in[:, :]).then_inc(s_w0, 16)
            eng.wait_ge(s_set, 4)
            for l, nt in ((0, NT0), (1, NT1)):
                for m in range(0, nt, 3):
                    eng.dma_start(xs[l][m * P:(m + 3) * P, :].rearrange("(t p) d -> p t d", p=P),
                                  zeros[:, 0:3 * D].rearrange("p (t d) -> p t d", t=3)).then_inc(s_zs, 16)

            def expert_rows(l, nt):
                def load(m, r):
                    eng.wait_ge(s_xT[l], m - RING + 1)
                    eng.dma_start(xt[:, r, :], xs[l][bass.ds(m * P, P), :]).then_inc(s_xload[l][r], 16)

                def store(m, r):
                    eng.wait_ge(s_yb[l], m + 1)
                    eng.dma_start(ys[l][bass.ds(m * P, P), :], yb[:, r, :]).then_inc(s_ystore[l][r], 16)

                eng.wait_ge(s_disp[l], 16 * NTOK)
                for r in range(RING):
                    eng.dma_start(xt[:, r, :], xs[l][r * P:(r + 1) * P, :]).then_inc(s_xload[l][r], 16)
                for m in range(2 * RING):
                    load(m + RING, m % RING)
                    if m >= 2:
                        store(m - 2, (m - 2) % RING)
                with eng.Fori(2, nt // RING - 1) as it:
                    for r in range(RING):
                        load(it * RING + (r + RING), r)
                        store(it * RING + (r - 2), (r - 2) % RING)
                for m in range(nt - RING - 2, nt):
                    store(m, m % RING)

            eng.wait_ge(s_out, len(jobs))
            eng.wait_ge(s_score, B * TB * H)
            eng.dma_start(wp1, wp1_in[:, :]).then_inc(s_w1, 16)
            expert_rows(0, NT0)
            expert_rows(1, NT1)
            for b in range(B):
                eng.wait_ge(s_fin, TB * (b + 1))
                eng.dma_start(out_view[:, b * TB:(b + 1) * TB, :], xc[:, b * TB:(b + 1) * TB, :]).then_inc(s_store, 16)
            eng.wait_ge(s_store, 16 * B)

        @block.gpsimd
        def _(eng):
            eng.memset(half[:, :], -0.5).then_inc(s_set, 1)
            eng.memset(qvT[:, :, S:QW], 0.0).then_inc(s_set, 1)
            eng.memset(qg[:, S:QW], 0.0).then_inc(s_set, 1)
            eng.memset(zeros[:, :], 0.0).then_inc(s_set, 1)
            eng.memset(qa[:, :, :], 0.0).then_inc(s_qz, 1)
            eng.wait_ge(s_set, 4)
            eng.wait_ge(s_qz, 1)
            steps = [0]

            def rsqrt(var, dst, width, scale, eps, need):
                eng.wait_ge(*need)
                if steps[0]:
                    eng.wait_ge(s_gstep, steps[0])
                eng.tensor_scalar(dst, var, scale, eps, ALU.mult, ALU.add).then_inc(s_gstep, 1)
                steps[0] += 1
                eng.wait_ge(s_gstep, steps[0])
                eng.tensor_tensor(dst, dst, half[:, 0:width], ALU.pow).then_inc(s_pow, 1)

            for e in plan:
                kind, b = e[0], e[1]
                if kind == "stats":
                    rsqrt(mv[:, 0, :, 1], rstd[:, 0, :], TB, 1.0, 1e-5, (s_var, variance[e]))
                    if b < 2:
                        eng.wait_ge(s_x[b], 16)
                    eng.tensor_tensor(xb[:, b * TB:(b + 1) * TB, :], xa[:, b * TB:(b + 1) * TB, :],
                                      A("bo").unsqueeze(1).broadcast_to([P, TB, D]), ALU.add).then_inc(s_xbo, 1)
                elif kind == "post":
                    rsqrt(mv[:, 1, :, 1], rstd[:, 1, :], TB, 1.0, 1e-5, (s_var, variance[e]))
                elif kind == "rms":
                    rsqrt(ssq[:, b * TB:(b + 1) * TB], rstd[:, 2, :], TB, 1.0 / D, 1e-6, (s_sq, TB * (b + 1)))
            nvar = len(variance)

            def move(l, rows_from, ready):
                eng.wait_ge(s_zs, 16 * ((NT0 + NT1) // 3))
                eng.wait_ge(*ready)
                for t in range(NTOK):
                    eng.indirect_dma_start(xs[l][:, :], bass.IndirectOffsetOnAxis(ap=pos[:, t:t + 1], axis=0),
                                           rows_from[:, t, :], None).then_inc(s_disp[l], 16)
                for r in range(RING):
                    eng.wait_ge(s_ystore[l][r], 16 * ((NT0, NT1)[l] // RING))

            def gather(l, b):
                for t in range(b * TB, (b + 1) * TB):
                    eng.indirect_dma_start(xa[:, t, :], None, ys[l][:, :],
                                           bass.IndirectOffsetOnAxis(ap=pos[:, t:t + 1], axis=0))\
                       .then_inc(s_gath[l][b], 16)

            def deviations(l, kind, b, k):
                tiles = slice(b * TB, (b + 1) * TB)
                rsqrt(mva[:, k, tiles, 1], rstda[:, k, tiles], TB, 1.0, 1e-5, (s_var, nvar + place_of[(l, kind, b)]))

            move(0, xc, (s_rt, 4))
            for kind, b in middle:
                r = b % 2
                if kind == "gather":
                    gather(0, b)
                elif kind in ("sum", "out"):
                    deviations(0, kind, b, 0)
                elif kind == "normed":
                    deviations(0, kind, b, 1)
                elif kind == "u":
                    for c in range(NC):
                        eng.wait_ge(s_uf, NC * b + c + 1)
                        eng.wait_ge(s_rsg, NC * b + c + 1)
                        eng.tensor_tensor(uu[:, r, c, :], uu[:, r, c, :], sg[:, r, c, :], ALU.mult).then_inc(s_u, 1)
                elif kind == "gate":
                    for c in range(NC):
                        eng.wait_ge(s_ract, 3 * (NC * b + c) + 2)
                        eng.tensor_tensor(gb[:, r, c, :], gb[:, r, c, :], uu[:, r, c, :], ALU.mult).then_inc(s_bu, 1)
                elif kind == "scan":
                    for c in range(NC):
                        eng.wait_ge(s_scan, NC * b + c + 1)
                        eng.wait_ge(s_ract, 3 * (NC * b + c) + 3)
                        eng.tensor_tensor(ga[:, r, c, :], ga[:, r, c, :], gc[:, r, c, :], ALU.mult).then_inc(s_cy, 1)
                        eng.wait_ge(s_cy, 2 * (NC * b + c) + 1)
                        eng.tensor_tensor(ga[:, r, c, :], ga[:, r, c, :], uu[:, r, c, :], ALU.add).then_inc(s_cy, 1)
            move(1, xb, (s_rt, 8))
            for kind, b in final:
                if kind == "gather":
                    gather(1, b)
                elif kind == "sum":
                    deviations(1, kind, b, 0)

        @block.scalar
        def _(eng):
            for kind, *w in plan:
                if kind == "score":
                    u = w[0]
                    b, i, h, g, j, m = uof(u)
                    eng.wait_ge(s_fixed, u + 1)
                    if u >= AHEAD:
                        eng.wait_ge(s_pT, u - AHEAD + 1)
                    if j == 0 and m >= 3:
                        eng.wait_ge(s_rinv, m - 2)
                    eng.activation(prob[:, u % AHEAD, :], SCORE[u % AHEAD][:, :], ACT.Exp, bias=nmax[:, u % AHEAD, :],
                                   accum_out=rsum[:, m % 3, j:j + 1]).then_inc(s_exp, 1)
                elif kind == "probs":
                    u = w[0]
                    eng.wait_ge(s_pT, u + 1)
                    if u >= 2:
                        eng.wait_ge(s_pv, u - 1)
                    eng.activation(probT[:, u % 2, :], PT[:, :], ACT.Copy).then_inc(s_pTs, 1)
                elif kind == "job" and jobs[w[0]][0] == "t2":
                    _, b, g = jobs[w[0]]
                    eng.wait_ge(s_qg, NG * b + g + 1)
                    eng.wait_ge(s_qz, 2)
                    if b:
                        eng.wait_ge(s_score, ((b - 1) * NG + g + 1) * TB * HG)
                    for j in range(HG):
                        rows = slice(HP * j, HP * (j + 1))
                        eng.activation(qa[rows, g * HG + j, :], qg[rows, 0:S], ACT.Copy).then_inc(s_qa, 1)
                elif kind == "rms":
                    b = w[0]
                    for t in range(b * TB, b * TB + TB):
                        eng.wait_ge(s_x1, t + 1)
                        if t:
                            eng.wait_ge(s_sq, t)
                        eng.activation(junk[:, :], xb[:, t, :], ACT.Square, accum_out=ssq[:, t:t + 1])\
                           .then_inc(s_sq, 1)

            def router_exp(l, E, need):
                eng.wait_ge(s_rt, need)
                eng.activation(rt[1][:, 0:NTOK * E], rt[0][:, 0:NTOK * E], ACT.Exp).then_inc(s_rte, 1)

            def experts(l, nt, F, func):
                CH = F // P

                def tile(m, r, first):
                    eng.wait_ge(s_h[l], m + 1)
                    if not first:
                        eng.wait_ge(s_y[l], m - (RING - 1))
                    for c in range(CH):
                        eng.activation(hT[:, r, c * P:(c + 1) * P], bank[r][:, c * P:(c + 1) * P], func,
                                       bias=wbuf[:, r, 2 * F + c:2 * F + c + 1]).then_inc(s_act[l], 1)

                for m in range(2 * RING):
                    tile(m, m % RING, m < RING)
                with eng.Fori(2, nt // RING) as it:
                    for r in range(RING):
                        tile(it * RING + r, r, False)

            router_exp(0, E0, 1)
            experts(0, NT0, F0, ACT.Silu)
            for kind, b in middle:
                r = b % 2
                if kind == "in":
                    for c in range(NC):
                        eng.wait_ge(s_rp, 2 * NC * b + c + 1)
                        if b >= 2:
                            eng.wait_ge(s_conv, NC * (b - 2) + c + 1)
                        eng.activation(pj[:, r, c, 2:2 + S], bank[c][:, :], ACT.Identity, bias=C("bin", c, 1))\
                           .then_inc(s_rpe, 1)
                    for c in range(NC):
                        eng.wait_ge(s_rp, 2 * NC * b + NC + c + 1)
                        if b >= 2:
                            eng.wait_ge(s_u, NC * (b - 2) + c + 1)
                        eng.activation(sg[:, r, c, :], bank[NC + c][:, :], ACT.Sigmoid, bias=C("bin", NC + c, 1))\
                           .then_inc(s_rsg, 1)
                elif kind == "conv":
                    for c in range(NC):
                        eng.wait_ge(s_conv, NC * b + c + 1)
                        if b >= 1:
                            eng.wait_ge(s_uf, NC * (b - 1) + c + 1)
                        eng.activation(sc[:, c, :], cv[:, c, :], ACT.Sigmoid, bias=C("cb", c, 1)).then_inc(s_rs, 1)
                elif kind == "gate":
                    for c in range(NC):
                        for q, (dst, f, bias) in enumerate(((ga, ACT.Sigmoid, "ba"), (gb, ACT.Sigmoid, "bb"),
                                                            (gc, ACT.Tanh, "bc"))):
                            eng.wait_ge(s_rg, 3 * (NC * b + c) + q + 1)
                            if b >= 2:
                                if q == 0:
                                    eng.wait_ge(s_ro, b - 1)
                                if q == 1:
                                    eng.wait_ge(s_scan, NC * (b - 2) + c + 1)
                                if q == 2:
                                    eng.wait_ge(s_cy, 2 * (NC * (b - 2) + c) + 1)
                            eng.activation(dst[:, r, c, :], bank[4 + (3 * (NC * b + c) + q) % 2][:, :], f,
                                           bias=C(bias, c, 1)).then_inc(s_ract, 1)
            router_exp(1, E1, 5)
            experts(1, NT1, F1, ACT.Gelu)

        @block.tensor
        def _(eng):
            ident = A("ident")
            eng.wait_ge(s_ca, 16)
            for kind, *w in plan:
                if kind == "score":
                    u = w[0]
                    b, i, h, g, j, m = uof(u)
                    if u >= AHEAD:
                        eng.wait_ge(s_exp, u - AHEAD + 1)
                    if u >= 1:
                        eng.wait_ge(s_diag, u)
                    if i == 0:
                        eng.wait_ge(s_qa, (NG * b + g) * HG + j + 1)
                        eng.wait_ge(s_qb, (NG * b + g) * HG + j + 1)
                    if u == 0:
                        eng.wait_ge(s_qz, 2)
                    lhs = slice(i * P, (i + 1) * P)
                    r = b % 2
                    if i:
                        eng.matmul(SCORE[u % AHEAD][:, 0:i * P], qa[:, h, lhs], ka[:, r, g, 0:i * P],
                                   start=True, stop=True)
                    eng.matmul(SCORE[u % AHEAD][:, i * P:S], qb[:, h, lhs], kb[:, r, g, i * P:S],
                               start=True, stop=True)
                    eng.matmul(DA[:, 0:P], qa[:, h, lhs], ka[:, r, g, i * P:(i + 1) * P],
                               start=True, stop=True).then_inc(s_score, 1)
                elif kind == "probs":
                    u = w[0]
                    eng.wait_ge(s_exp, u + 1)
                    if u >= 1:
                        eng.wait_ge(s_pTs, u)
                    for t in range(TB):
                        mm = eng.transpose(PT[:, t * P:(t + 1) * P], prob[:, u % AHEAD, t * P:(t + 1) * P], ident)
                    mm.then_inc(s_pT, 1)
                elif kind == "values":
                    u = w[0]
                    b, i, h, g, j, m = uof(u)
                    eng.wait_ge(s_pTs, u + 1)
                    if j == 0 and m >= 2:
                        eng.wait_ge(s_norm, m - 1)
                    for t in range(TB):
                        mm = eng.matmul(CTX[m % 2][HP * j:HP * (j + 1), 0:P],
                                        vv[:, b % 2, t, h * HP:(h + 1) * HP], probT[:, u % 2, t * P:(t + 1) * P],
                                        start=(t == 0), stop=(t == TB - 1))
                    mm.then_inc(s_pv, 1)
                elif kind == "job":
                    k = w[0]
                    name, *a = jobs[k]
                    bk = JOB
                    if k:
                        eng.wait_ge(s_out, k)

                    def after(*other):
                        eng.wait_ge(s_out, number[other] + 1)

                    if name == "pem":
                        mm = eng.matmul(bk[:, 0:H], A("wp"), A("pem"), start=True, stop=True)
                    elif name == "zT":
                        eng.wait_ge(s_z, TB * (a[0] + 1))
                        for t in range(TB):
                            mm = eng.transpose(bk[:, t * P:(t + 1) * P], z[:, t, :], ident)
                    elif name == "q":
                        after("zT", a[0])
                        mm = eng.matmul(bk[:, :], A("wq"), xnT[:, :], start=True, stop=True)
                    elif name == "k":
                        after("zT", a[0])
                        mm = eng.matmul(bk[:, :], A(f"wk{a[1]}"), xnT[:, :], start=True, stop=True)
                    elif name == "v":
                        after("zT", a[0])
                        for t in range(2):
                            at = (2 * a[1] + t) * P
                            mm = eng.matmul(bk[:, t * H * HP:(t + 1) * H * HP], xnT[:, at:at + P], A("wv"),
                                            start=True, stop=True)
                    elif name in ("t1", "t2"):
                        after("q", a[0])
                        mm = eng.matmul(bk[:, :], A(f"m{name[1]}_{a[1]}"), qvT[:, a[0] % 2, 0:S], start=True, stop=True)
                    elif name == "corr":
                        after("q", a[0])
                        after("pem", 0)
                        eng.wait_ge(s_set, 4)
                        for t in range(TB):
                            mm = eng.matmul(bk[:, t * H:(t + 1) * H], qvT[:, a[0] % 2, t * P + 1:(t + 1) * P + 1],
                                            pm1[:, :], start=True, stop=True)
                    elif name == "rT":
                        eng.wait_ge(s_rinv, a[0] + 1)
                        mm = eng.transpose(bk[:, 0:P], rinv[:, :], ident)
                    elif name == "out":
                        b, i = divmod(a[0], TB)
                        eng.wait_ge(s_norm, (b * NG + NG - 1) * TB + i + 1)
                        for g in range(NG):
                            mm = eng.matmul(bk[:, 0:D], cx[:, i, g, :], A(f"wo{g}"),
                                            start=(g == 0), stop=(g == NG - 1))
                    elif name == "xT":
                        eng.wait_ge(s_xn2, TB * (a[0] + 1))
                        for t in range(TB):
                            mm = eng.transpose(bk[:, t * P:(t + 1) * P], xc[:, a[0] * TB + t, :], ident)
                    elif name == "logits":
                        after("xT", a[0])
                        eng.wait_ge(s_cb, 16)
                        for t in range(TB):
                            mm = eng.matmul(bk[:, t * E0:(t + 1) * E0], xnT2[:, t * P:(t + 1) * P], C("gate"),
                                            start=True, stop=True)
                    mm.then_inc(s_job, 1)

            def counts(l, E):
                eng.wait_ge(s_rt, 4 * l + 2)
                eng.matmul(bank[0][:, 0:NTOK * E], C("upper"), rt[2][:, 0:NTOK * E], start=True, stop=True)\
                   .then_inc(s_rtp, 1)
                eng.matmul(bank[1][:, 0:NTOK * E], C("ones"), rt[2][:, 0:NTOK * E], start=True, stop=True)\
                   .then_inc(s_rtp, 1)

            def experts(l, nt, F):
                CH = F // P

                def transpose(m, r, it):
                    eng.wait_ge(s_xload[l][r], (it + 1) * 16)
                    if not (isinstance(m, int) and m == 0):
                        eng.wait_ge(s_xTs[l], m)
                    eng.transpose(bank[6][:, 0:P], xt[:, r, :], ident).then_inc(s_xT[l], 1)

                def hidden(m, r, first):
                    eng.wait_ge(s_xTs[l], m + 1)
                    eng.wait_ge(s_wb[l], m + 1)
                    if not first:
                        eng.wait_ge(s_act[l], (m - (RING - 1)) * CH)
                    for c in range(CH):
                        mm = eng.matmul(bank[r][:, c * P:(c + 1) * P], wbuf[:, r, c * P:(c + 1) * P], xTs[:, r, :],
                                        start=True, stop=True)
                    mm.then_inc(s_h[l], 1)

                def result(m, r, first):
                    eng.wait_ge(s_act[l], (m + 1) * CH)
                    if not first:
                        eng.wait_ge(s_yb[l], m - (RING - 1))
                    for c in range(CH):
                        mm = eng.matmul(bank[3 + r][:, 0:D], hT[:, r, c * P:(c + 1) * P],
                                        wbuf[:, r, F + c * D:F + (c + 1) * D], start=(c == 0), stop=(c == CH - 1))
                    mm.then_inc(s_y[l], 1)

                for m in range(2 * RING):
                    transpose(m, m % RING, m // RING)
                    if m >= 1:
                        hidden(m - 1, (m - 1) % RING, m - 1 < RING)
                    if m >= 2:
                        result(m - 2, (m - 2) % RING, m - 2 < RING)
                with eng.Fori(2, nt // RING) as it:
                    for r in range(RING):
                        transpose(it * RING + r, r, it)
                        hidden(it * RING + (r - 1), (r - 1) % RING, False)
                        result(it * RING + (r - 2), (r - 2) % RING, False)
                hidden(nt - 1, RING - 1, False)
                result(nt - 2, RING - 2, False)
                result(nt - 1, RING - 1, False)

            counts(0, E0)
            experts(0, NT0, F0)
            for kind, b in middle:
                r = b % 2
                if (kind, b) in turn and turn[(kind, b)] > 1:
                    eng.wait_ge(s_took, turn[(kind, b)] - 1)
                if kind == "in":
                    eng.wait_ge(s_z1, TB * (b + 1))
                    for t in range(TB):
                        mm = eng.transpose(bank[6][:, t * P:(t + 1) * P], z[:, t, :], ident)
                    mm.then_inc(s_turn, 1)
                    eng.wait_ge(s_took, turn[("in", b)])
                    for c in range(2 * NC):
                        if b and c < NC:
                            eng.wait_ge(s_rpe, NC * (b - 1) + c + 1)
                        if b and c >= NC:
                            eng.wait_ge(s_rsg, NC * (b - 1) + c - NC + 1)
                        eng.matmul(bank[c][:, :], C("win", c * P, P), xnT[:, :], start=True, stop=True)\
                           .then_inc(s_rp, 1)
                elif kind == "gate":
                    eng.wait_ge(s_u, NC * (b + 1))
                    for c in range(NC):
                        for q, name in enumerate(("wa", "wb", "wc")):
                            v = 3 * (NC * b + c) + q
                            if v >= 2:
                                eng.wait_ge(s_ract, v - 1)
                            for k in range(NC):
                                mm = eng.matmul(bank[4 + v % 2][:, :], C(name, k * INNER + c * P, P), uu[:, r, k, :],
                                                start=(k == 0), stop=(k == NC - 1))
                            mm.then_inc(s_rg, 1)
                elif kind == "out":
                    eng.wait_ge(s_cy, 2 * NC * (b + 1))
                    if b:
                        eng.wait_ge(s_res, b)
                    for t in range(TB):
                        eng.matmul(bank[7][:, t * P:(t + 1) * P], ident, C("bo1"), start=True, stop=False)
                        for k in range(NC):
                            mm = eng.matmul(bank[7][:, t * P:(t + 1) * P], ga[:, r, k, t * P:(t + 1) * P],
                                            C("wo1", k * D, D), start=False, stop=(k == NC - 1))
                    mm.then_inc(s_ro, 1)
                elif kind == "router":
                    eng.wait_ge(s_x3, TB * (b + 1))
                    for t in range(TB):
                        mm = eng.transpose(bank[6][:, t * P:(t + 1) * P], xb[:, b * TB + t, :], ident)
                    mm.then_inc(s_turn, 1)
                elif kind == "logits":
                    eng.wait_ge(s_took, turn[("router", b)])
                    for t in range(TB):
                        mm = eng.matmul(bank[6][:, t * E1:(t + 1) * E1], xnT2[:, t * P:(t + 1) * P], C("router"),
                                        start=True, stop=True)
                    mm.then_inc(s_turn, 1)
            counts(1, E1)
            experts(1, NT1, F1)

        @block.vector
        def _(eng):
            last = [None]
            tally = {}

            def count(s):
                tally[s.name] = tally.get(s.name, 0) + 1
                last[0] = (s, tally[s.name])
                return s

            def own():
                eng.wait_ge(*last[0])

            eng.memset(qb[:, :, :], 0.0).then_inc(count(s_qz), 1)
            eng.wait_ge(s_ca, 16)
            eng.tensor_tensor(col[:, 0:1], A("bq"), A("v"), ALU.add).then_inc(count(s_v), 1)
            for g in range(NG):
                eng.tensor_tensor(col[:, 1 + g:2 + g], A(f"u{g}"), A(f"v{g}"), ALU.subtract).then_inc(count(s_v), 1)

            def stats(rows, half_, sem_out):
                own()
                for t in range(TB):
                    eng.bn_stats(st[:, t, :], rows(t)).then_inc(count(s_v), 1)
                own()
                for t in range(TB):
                    eng.bn_aggr(mv[:, half_, t, :], st[:, t, :]).then_inc(count(sem_out if t == TB - 1 else s_v), 1)

            def normed(dst, rows, k, sem_each):
                own()
                for t in range(TB):
                    eng.tensor_scalar(dst(t), rows(t), mv[:, k, t, 0:1], rstd[:, k, t:t + 1], ALU.subtract, ALU.mult)\
                       .then_inc(count(sem_each), 1)

            for kind, *w in plan:
                if kind == "stats":
                    b = w[0]
                    if b < 2:
                        eng.wait_ge(s_x[b], 16)
                    stats(lambda t: xa[:, b * TB + t, :], 0, s_var)
                elif kind == "normz":
                    b = w[0]
                    if b:
                        eng.wait_ge(s_job, number[("zT", b - 1)] + 1)
                    eng.wait_ge(s_pow, power[("stats", b)])
                    normed(lambda t: z[:, t, :], lambda t: xa[:, b * TB + t, :], 0, s_z)
                elif kind == "score":
                    u = w[0]
                    b, i, h, g, j, m = uof(u)
                    sc_b = SCORE[u % AHEAD]
                    eng.wait_ge(s_score, u + 1)
                    eng.copy_predicated(sc_b[:, i * P:(i + 1) * P], A("tri").bitcast(U32), DA[:, 0:P])\
                       .then_inc(count(s_diag), 1)
                    own()
                    wide = min(P, S - 1 - i * P)
                    eng.scalar_tensor_tensor(out=sc_b[:, i * P + 1:i * P + 1 + wide], in0=A("ident")[:, 0:wide],
                                             scalar=corr[:, b % 2, i, h:h + 1],
                                             in1=sc_b[:, i * P + 1:i * P + 1 + wide],
                                             op0=ALU.mult, op1=ALU.add).then_inc(count(s_v), 1)
                    own()
                    if u >= AHEAD:
                        eng.wait_ge(s_exp, u - AHEAD + 1)
                    eng.tensor_reduce(nmax[:, u % AHEAD, :], sc_b[:, :], AX.X, ALU.max, negate=True)\
                       .then_inc(count(s_fixed), 1)
                elif kind == "recip":
                    m = w[0]
                    eng.wait_ge(s_exp, HG * (m + 1))
                    own()
                    eng.reciprocal(rone[:, :], rsum[:, m % 3, :]).then_inc(count(s_v), 1)
                    if m:
                        eng.wait_ge(s_job, number[("rT", m - 1)] + 1)
                    own()
                    eng.tensor_copy(rinv[:, :].rearrange("p (h d) -> p h d", h=HG),
                                    rone[:, :].unsqueeze(2).broadcast_to([P, HG, HP])).then_inc(count(s_rinv), 1)
                elif kind == "norm":
                    m = w[0]
                    b, g, i = m // (NG * TB), m // TB % NG, m % TB
                    own()
                    eng.wait_ge(s_pv, HG * (m + 1))
                    if b:
                        eng.wait_ge(s_job, number[("out", (b - 1) * TB + i)] + 1)
                    eng.tensor_tensor(cx[:, i, g, :], CTX[m % 2][:, 0:P], rT[:, :], ALU.mult)\
                       .then_inc(count(s_norm), 1)
                elif kind == "post":
                    b = w[0]
                    stats(lambda t: xb[:, b * TB + t, :], 1, s_var)
                elif kind == "post2":
                    b = w[0]
                    eng.wait_ge(s_pow, power[("post", b)])
                    normed(lambda t: xb[:, b * TB + t, :], lambda t: xb[:, b * TB + t, :], 1, s_x1)
                elif kind == "job":
                    k = w[0]
                    name, *a = jobs[k]
                    bk = JOB
                    if name == "xT":
                        b = a[0]
                        eng.wait_ge(s_cb, 16)
                        eng.wait_ge(s_pow, power[("rms", b)])
                        for t in range(TB):
                            eng.scalar_tensor_tensor(out=xc[:, b * TB + t, :], in0=xb[:, b * TB + t, :],
                                                     scalar=rstd[:, 2, t:t + 1], in1=C("rms"),
                                                     op0=ALU.mult, op1=ALU.mult).then_inc(count(s_xn2), 1)
                    own()
                    eng.wait_ge(s_job, k + 1)
                    if name == "pem":
                        eng.tensor_copy(pm1[:, :], bk[:, 0:H]).then_inc(count(s_out), 1)
                    elif name == "zT":
                        if a[0]:
                            eng.wait_ge(s_job, number[("v", a[0] - 1, 1)] + 1)
                        eng.tensor_scalar(xnT[:, :], bk[:, :], A("gamma"), A("beta"), ALU.mult, ALU.add)\
                           .then_inc(count(s_out), 1)
                    elif name == "q":
                        eng.tensor_scalar(qvT[:, a[0] % 2, 0:S], bk[:, :], col[:, 0:1], None, ALU.add)\
                           .then_inc(count(s_out), 1)
                    elif name == "k":
                        b, g = a
                        eng.wait_ge(s_ct, 16)
                        if b >= 2:
                            eng.wait_ge(s_score, (b - 1) * TB * H)
                        eng.scalar_tensor_tensor(out=ka[:, b % 2, g, :], in0=bk[:, :], scalar=A(f"bk{g}"),
                                                 in1=T(f"ka{g}"), op0=ALU.add, op1=ALU.add).then_inc(count(s_v), 1)
                        eng.scalar_tensor_tensor(out=kb[:, b % 2, g, :], in0=bk[:, :], scalar=A(f"bk{g}"),
                                                 in1=T(f"kb{g}"), op0=ALU.add, op1=ALU.add).then_inc(count(s_out), 1)
                    elif name == "v":
                        if a[0] >= 2:
                            eng.wait_ge(s_pv, (a[0] - 1) * TB * H)
                        eng.tensor_tensor(vv[:, a[0] % 2, 2 * a[1]:2 * a[1] + 2, :],
                                          bk[:, :].rearrange("p (t d) -> p t d", t=2),
                                          A("bv").unsqueeze(1).broadcast_to([P, 2, H * HP]), ALU.add)\
                           .then_inc(count(s_out), 1)
                    elif name == "t1":
                        eng.scalar_tensor_tensor(out=t1[:, :], in0=bk[:, :], scalar=col[:, 1 + a[1]:2 + a[1]],
                                                 in1=T(f"cos{a[1]}"), op0=ALU.add, op1=ALU.mult)\
                           .then_inc(count(s_out), 1)
                    elif name == "t2":
                        b, g = a
                        r = b % 2
                        eng.tensor_tensor(t2[:, :], bk[:, :], T(f"sin{g}"), ALU.mult).then_inc(count(s_out), 1)
                        own()
                        eng.wait_ge(s_set, 4)
                        if b or g:
                            eng.wait_ge(s_qa, (NG * b + g) * HG)
                        eng.tensor_tensor(qg[:, 0:S], t1[:, :], t2[:, :], ALU.add).then_inc(count(s_qg), 1)
                        own()
                        eng.tensor_scalar(t2[:, :], qg[:, 1:S + 1], A("pmask")[:, 0:1], None, ALU.mult)\
                           .then_inc(count(s_v), 1)
                        own()
                        if b:
                            eng.wait_ge(s_score, ((b - 1) * NG + g + 1) * TB * HG)
                        for j in range(HG):
                            rows = slice(HP * j, HP * (j + 1))
                            eng.scalar_tensor_tensor(out=qb[rows, g * HG + j, :], in0=qg[rows, 0:S],
                                                     scalar=A("pmask")[rows, 1:2], in1=t2[rows, :],
                                                     op0=ALU.mult, op1=ALU.add).then_inc(count(s_qb), 1)
                    elif name == "corr":
                        eng.tensor_copy(corr[:, a[0] % 2, :, :].rearrange("p t h -> p (t h)"), bk[:, 0:TB * H])\
                           .then_inc(count(s_out), 1)
                    elif name == "rT":
                        eng.tensor_copy(rT[:, :], bk[:, 0:P]).then_inc(count(s_out), 1)
                    elif name == "out":
                        eng.wait_ge(s_xbo, a[0] // TB + 1)
                        eng.tensor_tensor(xb[:, a[0], :], bk[:, 0:D], xb[:, a[0], :], ALU.add)\
                           .then_inc(count(s_out), 1)
                    elif name == "xT":
                        if a[0]:
                            eng.wait_ge(s_job, number[("logits", a[0] - 1)] + 1)
                        eng.tensor_copy(xnT2[:, :], bk[:, :]).then_inc(count(s_out), 1)
                    elif name == "logits":
                        b = a[0]
                        eng.tensor_copy(lg[:, b * TB * E0:(b + 1) * TB * E0], bk[:, 0:TB * E0])\
                           .then_inc(count(s_out), 1)

            def route(l, E, nt, width, logits):
                N = NTOK * E

                def ie(v):
                    return v[:, 0:N].rearrange("p (i e) -> p i e", e=E)

                def ei(v):
                    return v[:, 0:N].rearrange("p (e i) -> p i e", e=E)

                def over_e(v):
                    return v.unsqueeze(2).broadcast_to([P, NTOK, E])

                top, total, best, place = sm[:, 0, :], sm[:, 1, :], sm[:, 2, :], sm[:, 3, :]
                weight = sm[:, 4, :]
                ntile, upto = sm[:, 5, 0:E], sm[:, 0, 0:E]
                own()
                eng.tensor_reduce(top, ie(logits), AX.X, ALU.max).then_inc(count(s_v), 1)
                own()
                eng.tensor_tensor(ie(rt[0]), ie(logits), over_e(top), ALU.subtract).then_inc(count(s_rt), 1)
                own()
                eng.scalar_tensor_tensor(out=rt[3][:, 0:N], in0=rt[0][:, 0:N], scalar=0.0, in1=C(f"rev{l}"),
                                         op0=ALU.is_ge, op1=ALU.mult).then_inc(count(s_v), 1)
                own()
                eng.tensor_reduce(best, ie(rt[3]), AX.X, ALU.max).then_inc(count(s_v), 1)
                own()
                eng.tensor_tensor(ei(rt[2]), ie(rt[3]), over_e(best), ALU.is_equal).then_inc(count(s_rt), 1)
                eng.wait_ge(s_rte, l + 1)
                own()
                eng.tensor_reduce(total, ie(rt[1]), AX.X, ALU.add).then_inc(count(s_v), 1)
                own()
                eng.reciprocal(weight, total).then_inc(count(s_v), 1)
                eng.wait_ge(s_rtp, 2 * l + 2)
                own()
                eng.tensor_tensor_scan(rt[3][:, 0:N], C(f"run{l}"), bank[1][:, 0:N], 0.0, ALU.mult, ALU.add)\
                   .then_inc(count(s_v), 1)
                own()
                eng.tensor_tensor(rt[4][:, 0:N], rt[3][:, 0:N], bank[0][:, 0:N], ALU.add).then_inc(count(s_v), 1)
                own()
                eng.tensor_tensor(rt[4][:, 0:N], rt[4][:, 0:N], bank[1][:, 0:N], ALU.subtract).then_inc(count(s_v), 1)
                counts = rt[3][:, 0:N].rearrange("p (e i) -> p e i", e=E)[:, :, NTOK - 1:NTOK]
                eng.tensor_tensor(rt[1][:, 0:N].rearrange("p (e i) -> p e i", e=E),
                                  counts.broadcast_to([P, E, NTOK]),
                                  C(f"thr{l}").rearrange("p (e i) -> p e i", e=E), ALU.is_gt).then_inc(count(s_v), 1)
                own()
                eng.tensor_reduce(ntile, rt[1][:, 0:N].rearrange("p (e i) -> p e i", e=E), AX.X, ALU.add)\
                   .then_inc(count(s_v), 1)
                own()
                eng.tensor_tensor_scan(upto, C("ones", 0, E), ntile, 0.0, ALU.mult, ALU.add).then_inc(count(s_v), 1)
                own()
                ends = rt[1][0:1, 0:E * NTOK]
                M = nt * E
                eng.tensor_tensor(slotcmp[0:1, 0:M].rearrange("p (m e) -> p m e", e=E),
                                  sm[0:1, 0, 0:E].unsqueeze(1).broadcast_to([1, nt, E]),
                                  C(f"slot{l}", rows=slice(0, 1)).rearrange("p (m e) -> p m e", e=E), ALU.is_le)\
                   .then_inc(count(s_v), 1)
                own()
                eng.tensor_reduce(tex[:, 0:nt], slotcmp[0:1, 0:M].rearrange("p (m e) -> p m e", e=E), AX.X, ALU.add)\
                   .then_inc(count(s_v), 1)
                own()
                eng.tensor_scalar(offs[:, 0:nt], tex[:, 0:nt], float(E - 1), float(width), ALU.min, ALU.mult)\
                   .then_inc(count(s_rt), 1)
                eng.tensor_tensor(ntile, upto, ntile, ALU.subtract).then_inc(count(s_v), 1)
                own()
                eng.scalar_tensor_tensor(out=rt[3][:, 0:N].rearrange("p (e i) -> p e i", e=E),
                                         in0=ntile.unsqueeze(2).broadcast_to([P, E, NTOK]), scalar=float(P),
                                         in1=rt[4][:, 0:N].rearrange("p (e i) -> p e i", e=E),
                                         op0=ALU.mult, op1=ALU.add).then_inc(count(s_v), 1)
                own()
                eng.tensor_tensor(rt[4][:, 0:N], rt[3][:, 0:N], rt[2][:, 0:N], ALU.mult).then_inc(count(s_v), 1)
                own()
                eng.tensor_reduce(place, ei(rt[4]), AX.X, ALU.add).then_inc(count(s_v), 1)
                own()
                eng.tensor_copy(pos[:, :], place).then_inc(count(s_rt), 1)
                own()

            def experts(l, nt, F, width, wp):
                def fetch(m, r, first):
                    off = eng.value_load(offs[0:1, bass.ds(m, 1)], min_val=0, max_val=((E0, E1)[l] - 1) * width)
                    if not first:
                        eng.wait_ge(s_y[l], m - (RING - 1))
                        eng.wait_ge(s_yb[l], m - (RING - 1))
                    eng.tensor_copy(wbuf[:, r, 0:width], wp[:, bass.ds(off, width)]).then_inc(s_wb[l], 1)

                def turned(m, r, first):
                    eng.wait_ge(s_xT[l], m + 1)
                    if not first:
                        eng.wait_ge(s_h[l], m - (RING - 1))
                    eng.tensor_copy(xTs[:, r, :], bank[6][:, 0:P]).then_inc(s_xTs[l], 1)

                def result(m, r, turn, first):
                    eng.wait_ge(s_y[l], m + 1)
                    if not first:
                        eng.wait_ge(s_ystore[l][r], turn * 16)
                    eng.wait_ge(s_wb[l], m + 1)
                    eng.tensor_tensor(yb[:, r, :], bank[3 + r][:, 0:D], wbuf[:, r, 2 * F + F // P:width], ALU.add)\
                       .then_inc(s_yb[l], 1)

                eng.wait_ge(*((s_w0, 16), (s_w1, 16))[l])
                for m in range(2 * RING):
                    fetch(m, m % RING, m < RING)
                    turned(m, m % RING, m < RING)
                    if m >= 2:
                        result(m - 2, (m - 2) % RING, (m - 2) // RING, m - 2 < RING)
                with eng.Fori(2, nt // RING) as it:
                    for r in range(RING):
                        fetch(it * RING + r, r, False)
                        turned(it * RING + r, r, False)
                        result(it * RING + (r - 2), (r - 2) % RING, it if r == 2 else it - 1, False)
                for m in range(nt - 2, nt):
                    result(m, m % RING, m // RING, False)
                last[0] = (s_yb[l], nt)

            def stats_of(rows, k, tiles):
                own()
                for t in tiles:
                    eng.bn_stats(sta[:, t, :], rows[:, t, :]).then_inc(count(s_v), 1)
                own()
                for t in tiles:
                    eng.bn_aggr(mva[:, k, t, :], sta[:, t, :]).then_inc(count(s_var if t == tiles[-1] else s_v), 1)

            def normed_of(dst, rows, k, tiles, sem_each):
                own()
                for t in tiles:
                    eng.tensor_scalar(dst(t), rows[:, t, :], mva[:, k, t, 0:1], rstda[:, k, t:t + 1],
                                      ALU.subtract, ALU.mult).then_inc(count(sem_each), 1)

            def returned(l, b, tiles):
                eng.wait_ge(s_gath[l][b], 16 * TB)
                own()
                for t in tiles:
                    eng.scalar_tensor_tensor(out=xc[:, t, :], in0=xa[:, t, :], scalar=sm[:, 4, t:t + 1],
                                             in1=xb[:, t, :], op0=ALU.mult, op1=ALU.add).then_inc(count(s_v), 1)
                stats_of(xc, 0, tiles)

            npow = len(power)
            route(0, E0, NT0, WW0, lg)
            experts(0, NT0, F0, WW0, wp0)
            for r in range(2):
                for c in range(NC):
                    own()
                    eng.memset(pj[:, r, c, 0:2], 0.0).then_inc(count(s_v), 1)
            for kind, b in middle:
                r = b % 2
                tiles = range(b * TB, (b + 1) * TB)
                if kind == "sum":
                    returned(0, b, tiles)
                elif kind == "normed":
                    eng.wait_ge(s_pow, npow + place_of[(0, "sum", b)])
                    normed_of(lambda t: xc[:, t, :], xc, 0, tiles, s_v)
                    stats_of(xc, 1, tiles)
                elif kind == "z":
                    eng.wait_ge(s_pow, npow + place_of[(0, "normed", b)])
                    if b:
                        eng.wait_ge(s_turn, turn[("in", b - 1)])
                    normed_of(lambda t: z[:, t - b * TB, :], xc, 1, tiles, s_z1)
                elif kind == "in":
                    eng.wait_ge(s_turn, turn[("in", b)])
                    if b:
                        eng.wait_ge(s_rp, 2 * NC * b)
                    eng.tensor_scalar(xnT[:, :], bank[6][:, :], C("gamma1"), C("beta1"), ALU.mult, ALU.add)\
                       .then_inc(count(s_took), 1)
                elif kind == "conv":
                    for c in range(NC):
                        eng.wait_ge(s_rpe, NC * b + c + 1)
                        if b:
                            eng.wait_ge(s_rs, NC * (b - 1) + c + 1)
                        own()
                        eng.tensor_scalar(cv[:, c, :], pj[:, r, c, 0:S], C("cw", 3 * c, 1), None, ALU.mult)\
                           .then_inc(count(s_v), 1)
                        for k in (1, 2):
                            own()
                            eng.scalar_tensor_tensor(out=cv[:, c, :], in0=pj[:, r, c, k:k + S],
                                                     scalar=C("cw", 3 * c + k, 1), in1=cv[:, c, :],
                                                     op0=ALU.mult, op1=ALU.add)\
                               .then_inc(count(s_conv if k == 2 else s_v), 1)
                elif kind == "u":
                    for c in range(NC):
                        eng.wait_ge(s_rs, NC * b + c + 1)
                        if b >= 2:
                            eng.wait_ge(s_cy, 2 * NC * (b - 1))
                            eng.wait_ge(s_rg, 3 * NC * (b - 1))
                        own()
                        eng.scalar_tensor_tensor(out=uu[:, r, c, :], in0=cv[:, c, :], scalar=C("cb", c, 1),
                                                 in1=sc[:, c, :], op0=ALU.add, op1=ALU.mult).then_inc(count(s_uf), 1)
                elif kind == "scan":
                    for c in range(NC):
                        eng.wait_ge(s_bu, NC * b + c + 1)
                        own()
                        eng.tensor_tensor_scan(ga[:, r, c, :], ga[:, r, c, :], gb[:, r, c, :], 0.0, ALU.mult, ALU.add)\
                           .then_inc(count(s_scan), 1)
                elif kind == "out":
                    eng.wait_ge(s_ro, b + 1)
                    own()
                    eng.scalar_tensor_tensor(out=xb[:, b * TB:(b + 1) * TB, :], in0=xc[:, b * TB:(b + 1) * TB, :],
                                             scalar=2.0, in1=bank[7][:, :].rearrange("p (t d) -> p t d", t=TB),
                                             op0=ALU.mult, op1=ALU.add).then_inc(count(s_res), 1)
                    stats_of(xb, 0, tiles)
                elif kind == "x3":
                    eng.wait_ge(s_pow, npow + place_of[(0, "out", b)])
                    normed_of(lambda t: xb[:, t, :], xb, 0, tiles, s_x3)
                elif kind == "router":
                    eng.wait_ge(s_turn, turn[(kind, b)])
                    if b:
                        eng.wait_ge(s_turn, turn[("logits", b - 1)])
                    own()
                    eng.tensor_copy(xnT2[:, :], bank[6][:, :]).then_inc(count(s_took), 1)
                elif kind == "logits":
                    eng.wait_ge(s_turn, turn[(kind, b)])
                    own()
                    eng.tensor_copy(lg[:, b * TB * E1:(b + 1) * TB * E1], bank[6][:, 0:TB * E1])\
                       .then_inc(count(s_took), 1)
            route(1, E1, NT1, WW1, lg)
            experts(1, NT1, F1, WW1, wp1)
            for kind, b in final:
                tiles = range(b * TB, (b + 1) * TB)
                if kind == "sum":
                    returned(1, b, tiles)
                elif kind == "normed":
                    eng.wait_ge(s_pow, npow + place_of[(1, "sum", b)])
                    normed_of(lambda t: xc[:, t, :], xc, 0, tiles, s_fin)


def kernel(**inputs):
    import concourse.bacc as bacc
    from concourse.bass_utils import run_bass_kernel_spmd

    a = {k: np.asarray(v) for k, v in inputs.items()}
    f32 = np.float32
    eye = np.eye(P, dtype=f32)
    div = np.exp(np.arange(0, D, 2, dtype=f32) * f32(-np.log(10000.0) / D)).astype(np.float64)
    k = np.arange(S, dtype=np.float64)

    def diagonal(w, transposed=False):
        m = np.zeros((P, P), f32)
        for h in range(H):
            m[h * DH:(h + 1) * DH, h * DH:(h + 1) * DH] = w.T if transposed else w
        return m

    def column(v):
        return np.reshape(v, (-1, 1))

    def across(v):
        return np.broadcast_to(np.reshape(v, (1, -1)), (P, v.size))

    fa = {"ident": eye, "tri": np.tril(np.ones((P, P), f32)), "wq": diagonal(a["L0_attn_Wq"]),
          "wp": diagonal(a["L0_attn_Wp"]),
          "gamma": column(a["L0_attn_ln_gamma"]), "beta": column(a["L0_attn_ln_beta"]),
          "bq": column(np.tile(a["L0_attn_bq"], H)), "v": column(a["L0_attn_v_bias"]),
          "bo": across(a["L0_attn_bo"])}
    wv, bv, wo = np.zeros((P, H, HP), f32), np.zeros((H, HP), f32), np.zeros((H, HP, D), f32)
    for h in range(H):
        wv[h * DH:(h + 1) * DH, h, 0:DH] = a["L0_attn_Wv"]
        bv[h, 0:DH] = a["L0_attn_bv"]
        wo[h, 0:DH] = a["L0_attn_Wo"][h * DH:(h + 1) * DH]
    wo = wo.reshape(NG, P, D)
    fa |= {"wv": wv, "bv": across(bv), "wo0": wo[0], "wo1": wo[1]}
    ft = {}
    pem, pmask = np.zeros((P, H), f32), np.zeros((P, 2), f32)
    for h in range(H):
        w = div[h * DH // 2:(h + 1) * DH // 2]
        pem[h * DH:(h + 1) * DH:2, h] = SCALE * np.sin(w)
        pem[h * DH + 1:(h + 1) * DH:2, h] = -SCALE * np.cos(w)
    for g in range(NG):
        wk, m1, m2 = (np.zeros((P, P), f32) for _ in range(3))
        cols = {n: np.zeros((P, 1), f32) for n in ("bk", "u", "v")}
        cos, sin, ka, kb = np.full((P, S), SCALE, f32), np.zeros((P, S), f32), np.zeros((P, S), f32), np.zeros((P, S), f32)
        for j in range(HG):
            h = g * HG + j
            src, con, posn = slice(h * DH, (h + 1) * DH), slice(32 * j, 32 * j + DH), slice(32 * j + DH, 32 * j + 2 * DH)
            wk[src, con] = a["L0_attn_Wk"]
            m1[src, con] = np.eye(DH)
            m1[src, posn] = a["L0_attn_Wp"].T
            m2[src, posn] = a["L0_attn_Wp"].reshape(DH // 2, 2, DH)[:, ::-1].reshape(DH, DH).T
            cols["bk"][con, 0] = a["L0_attn_bk"]
            cols["u"][con, 0] = a["L0_attn_u_bias"][h]
            cols["v"][con, 0] = a["L0_attn_v_bias"][h]
            w = div[h * DH // 2:(h + 1) * DH // 2, None]
            s0, c0 = posn.start, posn.start + 1
            cos[s0:posn.stop:2] = SCALE * np.cos(w * k)
            cos[c0:posn.stop:2] = SCALE * np.cos(w * k)
            sin[s0:posn.stop:2] = SCALE * np.sin(w * k)
            sin[c0:posn.stop:2] = -SCALE * np.sin(w * k)
            for table, shift in ((ka, S - 1), (kb, -1)):
                table[s0:posn.stop:2] = np.sin(w * (k + shift))
                table[c0:posn.stop:2] = np.cos(w * (k + shift))
            pmask[posn, 0] = 1.0
            pmask[con, 1] = 1.0
        fa |= {f"wk{g}": wk, f"m1_{g}": m1, f"m2_{g}": m2, f"bk{g}": cols["bk"], f"u{g}": cols["u"], f"v{g}": cols["v"]}
        ft |= {f"cos{g}": cos, f"sin{g}": sin, f"ka{g}": ka, f"kb{g}": kb}
    fa |= {"pem": pem, "pmask": pmask}

    def chunks(w, n):
        return w.reshape(n, P, -1).transpose(1, 0, 2).reshape(P, -1)

    fb = {"upper": np.triu(np.ones((P, P), f32), 1), "ones": np.ones((P, P), f32), "rms": across(a["L0_ffn_rms_w"]),
          "gate": a["L0_ffn_gate_w"].T, "router": a["L1_ffn_router_w"], "bo1": across(a["L1_attn_bo"]),
          "gamma1": column(a["L1_attn_gamma"]), "beta1": column(a["L1_attn_beta"]), "win": a["L1_attn_W_in"],
          "bin": a["L1_attn_b_in"].reshape(2 * NC, P).T, "cw": chunks(a["L1_attn_conv_w"].reshape(INNER, 3), NC),
          "cb": a["L1_attn_conv_b"].reshape(NC, P).T, "wo1": chunks(a["L1_attn_Wo"], NC)}
    for n in "abc":
        fb["w" + n] = chunks(a["L1_attn_W" + n], NC)
        fb["b" + n] = a["L1_attn_b" + n].reshape(NC, P).T
    for l, (E, nt) in enumerate(((E0, NT0), (E1, NT1))):
        fb[f"rev{l}"] = across(np.tile(np.arange(E, 0, -1), NTOK))
        fb[f"run{l}"] = across(np.tile(np.arange(NTOK) > 0, E))
        fb[f"thr{l}"] = across(np.tile(P * np.arange(NTOK), E))
        fb[f"slot{l}"] = across(np.repeat(np.arange(nt), E))

    def packed(fields, values):
        return np.concatenate([np.asarray(values[n], f32).reshape(P, w) for n, w in fields], axis=1)

    def experts(w1, b1, w2, b2):
        E, _, F = w1.shape
        return np.concatenate([w1.transpose(1, 0, 2), w2.reshape(E, F // P, P, D).transpose(2, 0, 1, 3).reshape(P, E, -1),
                               b1.reshape(E, F // P, P).transpose(2, 0, 1), np.broadcast_to(b2[None], (P, E, D))],
                              axis=2).reshape(P, -1)

    arrays = {"x": a["L0_attn_inputs"], "ca": packed(FIELDS_A, fa), "ct": packed(FIELDS_T, ft), "cb": packed(FIELDS_B, fb),
              "wp0": experts(*(a["L0_ffn_" + n] for n in ("W1", "b1", "W2", "b2"))),
              "wp1": experts(*(a["L1_ffn_" + n] for n in ("w1", "b1", "w2", "b2")))}
    arrays = {n: np.ascontiguousarray(v) for n, v in arrays.items()}
    nc = bacc.Bacc("TRN2", target_bir_lowering=False, num_devices=1)
    args = [nc.dram_tensor(n + "_in", v.shape, F32, kind="ExternalInput").ap() for n, v in arrays.items()]
    args.append(nc.dram_tensor("out", (B, S, D), F32, kind="ExternalOutput").ap())
    build(nc, *args)
    r = run_bass_kernel_spmd(nc, [{n + "_in": v for n, v in arrays.items()}], core_ids=[0])
    return r.results[0]["out"]
```
